# Optimizing a Trainium2 kernel written in Bass

```python
import numpy as np
import jax
import jax.numpy as jnp

def _softmax(x, axis=-1):
    return jax.nn.softmax(x, axis=axis)

def _gelu(x):
    return jax.nn.gelu(x, approximate=True)

def _silu(x):
    return jax.nn.silu(x)

def _sigmoid(x):
    return jax.nn.sigmoid(x)

def _layernorm(x, axis=-1, eps=1e-05):
    m = jnp.mean(x, axis=axis, keepdims=True)
    v = jnp.var(x, axis=axis, keepdims=True)
    return (x - m) / jnp.sqrt(v + eps)

def _scatter_add(tgt, idx, src, axis=0):
    return tgt.at[idx].add(src)

def _segment_sum(src, seg, n):
    return jax.ops.segment_sum(src, seg, n)
kernel_name = 'mk_prb_d1_jaxref_r8_367c42'

def setup_inputs(seed: int=0):
    np.random.seed(seed)
    _w = jnp.asarray

    def _L0_attn_setup():
        import jax, jax.numpy as jnp
        import numpy as np
        EMBED_DIM = 128
        NUM_HEADS = 16
        D_K = EMBED_DIM // NUM_HEADS
        B, T = (4, 256)
        key = jax.random.key(seed)
        k_x, k_wqkv, k_wo = jax.random.split(key, 3)
        x = jax.random.normal(k_x, (B, T, EMBED_DIM), dtype=jnp.float32)
        std = np.sqrt(2.0 / EMBED_DIM).astype(np.float32)
        W_qkv = jax.random.normal(k_wqkv, (EMBED_DIM, 3 * EMBED_DIM), dtype=jnp.float32) * std
        b_qkv = jnp.zeros((3 * EMBED_DIM,), dtype=jnp.float32)
        W_o = jax.random.normal(k_wo, (EMBED_DIM, EMBED_DIM), dtype=jnp.float32) * std
        b_o = jnp.zeros((EMBED_DIM,), dtype=jnp.float32)
        return {'x': x, 'W_qkv': W_qkv, 'b_qkv': b_qkv, 'W_o': W_o, 'b_o': b_o}
    _L0_attn_in = _L0_attn_setup()

    def _L0_ffn_setup():
        import jax, jax.numpy as jnp
        import numpy as np
        B, S, D, F, E, K = (2, 256, 128, 256, 8, 2)
        key = jax.random.key(seed)
        ks = jax.random.split(key, 5)
        scale = 0.02
        return {'x': jax.random.normal(ks[0], (B, S, D), dtype=jnp.float32), 'Wg': jax.random.normal(ks[1], (E, D), dtype=jnp.float32) * scale, 'W1': jax.random.normal(ks[2], (E, F, D), dtype=jnp.float32) * scale, 'W2': jax.random.normal(ks[3], (E, F, D), dtype=jnp.float32) * scale, 'W3': jax.random.normal(ks[4], (E, D, F), dtype=jnp.float32) * scale}
    _L0_ffn_in = _L0_ffn_setup()
    _d = {'L0_attn_x': _L0_attn_in['x'], 'L0_attn_W_qkv': _L0_attn_in['W_qkv'], 'L0_attn_b_qkv': _L0_attn_in['b_qkv'], 'L0_attn_W_o': _L0_attn_in['W_o'], 'L0_attn_b_o': _L0_attn_in['b_o'], 'L0_ffn_Wg': _L0_ffn_in['Wg'], 'L0_ffn_W1': _L0_ffn_in['W1'], 'L0_ffn_W2': _L0_ffn_in['W2'], 'L0_ffn_W3': _L0_ffn_in['W3']}
    _x0 = _d['L0_attn_x']
    _d['L0_attn_x'] = jax.random.normal(jax.random.fold_in(jax.random.key(seed), 1), (4, 512, 128), dtype=_x0.dtype)
    del _x0
    return _d

def reference(L0_attn_x, L0_attn_W_qkv, L0_attn_b_qkv, L0_attn_W_o, L0_attn_b_o, L0_ffn_Wg, L0_ffn_W1, L0_ffn_W2, L0_ffn_W3):

    def _L0_attn_ref(x, W_qkv, b_qkv, W_o, b_o):
        import jax, jax.numpy as jnp
        import numpy as np
        EMBED_DIM = 128
        NUM_HEADS = 16
        D_K = EMBED_DIM // NUM_HEADS
        B, T = (4, 256)
        Bsz, Tlen, D = x.shape
        qkv = x @ W_qkv + b_qkv
        q, k, v = jnp.split(qkv, 3, axis=-1)

        def heads(t):
            return t.reshape(Bsz, Tlen, NUM_HEADS, D_K).transpose(0, 2, 1, 3)
        q, k, v = (heads(q), heads(k), heads(v))
        scores = jnp.einsum('bhqd,bhkd->bhqk', q, k) / jnp.sqrt(jnp.float32(D_K))
        causal = jnp.tril(jnp.ones((Tlen, Tlen), dtype=bool))
        scores = jnp.where(causal[None, None], scores, -jnp.inf)
        attn = jax.nn.softmax(scores, axis=-1)
        out = jnp.einsum('bhqk,bhkd->bhqd', attn, v)
        out = out.transpose(0, 2, 1, 3).reshape(Bsz, Tlen, D)
        return out @ W_o + b_o

    def _L0_ffn_ref(x, Wg, W1, W2, W3):
        import jax, jax.numpy as jnp
        import numpy as np
        B, S, D, F, E, K = (2, 256, 128, 256, 8, 2)
        k = K
        scores = jnp.einsum('bsd,ed->bse', x, Wg)
        topk_scores, topk_idx = jax.lax.top_k(scores, k)
        topk_probs = jax.nn.softmax(topk_scores, axis=-1)
        h1 = jnp.einsum('bsd,efd->bsef', x, W1)
        h2 = jnp.einsum('bsd,efd->bsef', x, W2)
        hidden = jax.nn.silu(h1) * h2
        expert_out = jnp.einsum('bsef,edf->bsed', hidden, W3)
        onehot = jax.nn.one_hot(topk_idx, scores.shape[-1], dtype=x.dtype)
        gating = jnp.einsum('bsk,bske->bse', topk_probs, onehot)
        return jnp.einsum('bse,bsed->bsd', gating, expert_out)
    x = L0_attn_x
    xn = _layernorm(x, axis=-1)
    x = x + _L0_attn_ref(xn, L0_attn_W_qkv, L0_attn_b_qkv, L0_attn_W_o, L0_attn_b_o) + _L0_ffn_ref(xn, L0_ffn_Wg, L0_ffn_W1, L0_ffn_W2, L0_ffn_W3)
    return x

_drawn_inputs = setup_inputs


def setup_inputs(seed=0):
    import zlib

    import numpy as np

    out = dict(_drawn_inputs(seed))
    spreads = {'L0_attn_b_qkv': (0.0, 0.1), 'L0_attn_b_o': (0.0, 0.345)}
    factors = {'L0_ffn_Wg': 8.0, 'L0_ffn_W1': 8.0, 'L0_ffn_W2': 8.0, 'L0_ffn_W3': 8.0}
    for name, (base, spread) in spreads.items():
        noise = np.random.default_rng([zlib.crc32(name.encode()), seed]).standard_normal(out[name].shape)
        drawn = base * np.exp(spread * noise) if base else spread * noise
        out[name] = jnp.asarray(drawn.astype(out[name].dtype))
    for name, factor in factors.items():
        out[name] = (out[name] * factor).astype(out[name].dtype)
    return out
```

```python
from contextlib import ExitStack

import concourse.bass as bass
from concourse import mybir

ALU = mybir.AluOpType
ACT = mybir.ActivationFunctionType
AX = mybir.AxisListType
F32 = mybir.dt.float32
BF16 = mybir.dt.bfloat16
I32 = mybir.dt.int32
U32 = mybir.dt.uint32

P = 128
HEADS = 16
DK = 8
QUAD = 4
EXPERTS = 8
TOP = 2
EPS = 1e-5
MASKED = -3.0e38

Q_PART = (0, 0, 0, 1, 1, 2)
K_PART = (0, 1, 2, 0, 1, 0)
TERM_ROWS = len(Q_PART) * DK
SHIFT_ROW = 64
SHIFT_PARTS = 3
VW = 16
ROWS = 96

CHUNKS = (((0, 0, 0),), ((1, 0, 0),), ((0, 1, 0), (0, 3, 384)), ((1, 1, 0), (1, 3, 384)), ((0, 2, 0), (1, 2, 256)))
DIAGONALS = ((0, 512, 5), (1408, 512, 2), (2304, 512, 1))
MAX_GROUPS = tuple((3, c, 1) for c in range(4)) + tuple((2, c, 1) for c in range(4)) + ((1, 0, 2), (1, 2, 2), (0, 0, 4))
NMAX = len(MAX_GROUPS)
NEXP = 2 * len(CHUNKS)


def chunk_of(c, j):
    for n, parts in enumerate(CHUNKS):
        for head, tile, col in parts:
            if (head, tile) == (c % 2, j):
                return 5 * (c // 2) + n, col


def attention_and_experts(nc, x, w_qkv, b_qkv, bqk_t, w_o, b_o, wg_t, w12_t, w3_t, out):
    B, T, D = x.shape
    F = w12_t.shape[2] // 2
    TILES = T // P
    NT = B * TILES
    QUADS = HEADS // QUAD
    STEPS = B * QUADS
    FC = F // P
    SLOTS = NT * P * TOP
    NBLK = SLOTS // P + EXPERTS - 1
    SCALE = float(DK) ** -0.5
    assert D == P and T == 512 and HEADS * DK == D and FC == 2

    with ExitStack() as ctx:
        def sb(name, shape, dt=F32):
            return ctx.enter_context(nc.sbuf_tensor(name, shape, dt))

        def bank(name):
            return ctx.enter_context(nc.psum_tensor(name, [P, 512], F32))

        def sem(name):
            return ctx.enter_context(nc.semaphore(name))

        qk_dram = nc.dram_tensor("qk_parts_dram", [B, P, 2, 3, T], BF16).ap()
        xs_dram = nc.dram_tensor("sorted_x_dram", [NBLK * P, D], F32).ap()
        ys_dram = nc.dram_tensor("sorted_y_dram", [NBLK * P, D], F32).ap()

        OTS = QUADS + 1
        wqkv = sb("wqkv", [P, 3 * D])
        wvg = sb("wvg", [P, D + EXPERTS])
        wo = sb("wo", [P, D])
        w12 = sb("w12", [P, EXPERTS, 2 * F])
        w3 = sb("w3", [P, EXPERTS, FC, D])
        bq = sb("bq", [P, 2])
        bv_row = sb("bv_row", [P, D])
        bo_row = sb("bo_row", [P, D])
        ident = sb("ident", [P, P])
        ident_bf = sb("ident_bf", [P, P], BF16)
        ones_bf = sb("ones_bf", [P, P], BF16)
        before = sb("before", [P, P], BF16)
        future = sb("future", [P, P], BF16)
        iota_e = sb("iota_e", [P, EXPERTS])
        iota_128 = sb("iota_128", [P, NT])
        iota_blk = sb("iota_blk", [P, NBLK])
        tri_e = sb("tri_e", [P, EXPERTS, EXPERTS])
        zeros = sb("zeros", [P, 1024])
        xt = sb("xt", [P, NT, D])
        xn = sb("xn", [P, NT, D])
        xa = sb("xa", [P, NT, D])
        xnT = sb("xnT", [P, B, T])
        stats = sb("stats", [P, NT, 6])
        mv = sb("mv", [P, NT, 2])
        ve = sb("ve", [P, NT])
        sd = sb("sd", [P, NT])
        rstd = sb("rstd", [P, NT])
        nmr = sb("nmr", [P, NT])
        early = sb("early", [P, 6 * T])
        qkf = early[:, 0:4 * T].rearrange("p (n w t) -> p n w t", n=2, w=2)
        rest = early[:, 4 * T:6 * T].rearrange("p (w t) -> p w t", w=2)
        parts = sb("parts", [P, 2, 2, 3, T], BF16)
        qx = sb("qx", [P, QUADS, QUAD, T], BF16)
        kx = sb("kx", [P, QUADS, QUAD, T], BF16)
        v = sb("v", [P, B, TILES, HEADS, VW])
        nmax = sb("nmax", [P, 2, QUAD, TILES])
        nmr_rows = sb("nmr_rows", [TILES * QUAD, 2, P])
        nm_rest = sb("nm_rest", [TILES * QUAD, 2, P])
        nm_parts = sb("nm_parts", [TILES * QUAD, 2, 3, P], BF16)
        probs = sb("probs", [P, 2, NEXP * 512])
        ot = sb("ot", [P, OTS, T])
        rden = sb("rden", [P, HEADS])
        on = sb("on", [P, TILES, D])
        onT = sb("onT", [P, TILES * P])
        sc = sb("sc", [P, NT, EXPERTS])
        mx = sb("mx", [P, NT, 8])
        ix = sb("ix", [P, NT, 8], U32)
        ixf = sb("ixf", [P, NT, TOP])
        onehot = sb("onehot", [P, NT * TOP, EXPERTS], BF16)
        dsc = sb("dsc", [P, NT])
        esc = sb("esc", [P, NT])
        prob = sb("prob", [P, TOP, NT])
        cnt = sb("cnt", [P, EXPERTS], BF16)
        total = sb("total", [P, EXPERTS])
        over = sb("over", [P, EXPERTS, NT])
        nblk = sb("nblk", [P, EXPERTS])
        first = sb("first", [P, EXPERTS])
        last = sb("last", [P, EXPERTS])
        first128 = sb("first128", [P, EXPERTS])
        tri_t = sb("tri_t", [P, EXPERTS, EXPERTS])
        rank = sb("rank", [P, NT * TOP, EXPERTS])
        posf = sb("posf", [P, NT * TOP])
        pos = sb("pos", [P, NT * TOP], U32)
        past = sb("past", [P, NBLK, EXPERTS])
        ebf = sb("ebf", [P, NBLK])
        eb = sb("eb", [P, NBLK], I32)
        NXS = 4
        xs = sb("xs", [P, NXS, D])
        fx = early[:, 0:3 * 512].rearrange("p (n f) -> p n f", n=3)
        th = sb("th", [P, F])
        hid = sb("hid", [P, 2, F])
        yg = early[:, 3 * 512:3 * 512 + 4 * TOP * D].rearrange("p (n c d) -> p n c d", n=4, c=TOP)
        acc = early[:, 5 * 512:6 * 512].rearrange("p (n d) -> p n d", n=4)

        SM = [bank(f"SM{i}") for i in range(2)]
        ST = [bank(f"ST{i}") for i in range(2)]
        PO = bank("PO")
        M = bank("M")
        FH = bank("FH")
        FM = bank("FM")

        s_x = [sem(f"x_in{b}") for b in range(B)]
        s_w = sem("w_in")
        s_wf = sem("ffn_w_in")
        s_const = sem("const_done")
        s_pc = sem("pool_chain")
        s_zero = sem("zeros_done")
        s_wvg = sem("wvg_done")
        s_dc = sem("dve_chain")
        s_ve = sem("var_done")
        s_sd = sem("sd_done")
        s_rstd = sem("rstd_done")
        s_xn = sem("xn_done")
        s_xa = sem("xa_done")
        s_m = sem("misc_written")
        s_mf = sem("misc_read")
        s_part = sem("parts_done")
        s_rest = sem("rest_done")
        s_bounce = [sem(f"parts_in_dram{b}") for b in range(B)]
        s_slot = [sem(f"qkx_in{g}") for g in range(QUADS)]
        s_shift = [sem(f"shift_in{g}") for g in range(QUADS)]
        s_kxz = sem("qkx_cleared")
        s_v = sem("v_done")
        s_v1 = sem("v_ones_done")
        s_sm = sem("scores_written")
        s_max = sem("max_done")
        s_nm = sem("negmax_parts")
        s_st = sem("scoresT_written")
        s_exp = sem("exp_done")
        s_sel = sem("causal_done")
        s_po = sem("pv_written")
        s_poz = sem("pv_cleared")
        s_ot = sem("pv_read")
        s_oh = sem("onehot_done")
        s_ds = sem("score_gap_done")
        s_es = sem("score_gap_exp")
        s_rank = sem("rank_written")
        s_pos = sem("pos_done")
        s_eb = sem("block_expert_done")
        s_xz = sem("sorted_x_cleared")
        s_xs_out = sem("sorted_x_out")
        s_xs = [sem(f"block_in{i}") for i in range(NXS)]
        s_f1 = sem("ffn_mid_written")
        s_fx = sem("ffn_mid_read")
        s_fh = sem("h_written")
        s_th = sem("tanh_done")
        s_hid = sem("hidden_done")
        s_ys = [sem(f"y_out{i}") for i in range(3)]
        s_yg = [sem(f"y_in{i}") for i in range(4)]
        s_res = sem("result_done")
        s_out = sem("out_written")

        UNITS = NBLK + 3
        FIRST_FFN = 4
        beside = {(s, k): [] for s in range(-1, STEPS + 2) for k in range(NMAX)}
        for b in range(1, B):
            beside[(0, 3 * b - 3)].append(("xnT", b))
            beside[(0, 3 * b - 2)].append(("q", b))
            beside[(0, 3 * b - 2)].append(("k", b))
            beside[(0, 3 * b - 1)].append(("v", b, 0))
            beside[(0, 3 * b)].append(("v", b, 1))
        beside[(1, 1)].append(("route",))
        for s in range(STEPS):
            beside[(s, 10)].append(("shift", s + 1))
            beside[(s, 4)].append(("pv", s - 1))
        beside[(STEPS, 0)].append(("pv", STEPS - 1))
        for b in range(B):
            s = QUADS * b + QUADS + 1
            for i in range(TILES):
                beside[(s, 1 + 2 * i if s < STEPS + 1 else 0)].append(("otT", b, i))
            beside[(s, 9 if s < STEPS + 1 else 1)].append(("onT", b))
            beside[(s, 10 if s < STEPS + 1 else 2)].append(("wo", b))
        spots = [(s, k) for s in range(FIRST_FFN, STEPS) for k in (0, 3, 6, 9)]
        for u in range(UNITS):
            beside[spots[u] if u < len(spots) else (STEPS, 3)].append(("ffn", u))
        order = [("xnT", 0), ("q", 0), ("k", 0), ("v", 0, 0), ("v", 0, 1), ("max", 0), ("shift", 0)]
        for s in range(0, STEPS + 2):
            for k in range(NMAX):
                if s + 1 < STEPS:
                    order.append(("max1", s + 1, k))
                if s < STEPS and k < NEXP:
                    order.append(("exp1", s, k))
                order += [w for w in beside[(s, k)] if not (w[0] == "shift" and w[1] >= STEPS) and not (w[0] == "pv" and w[1] < 0)]
        flat = []
        for w in order:
            flat += [("max1", w[1], k) for k in range(NMAX)] if w[0] == "max" else [w]
        order = flat
        MISC = ("xnT", "q", "k", "v", "shift", "otT", "onT", "wo")
        turn = {w: n for n, w in enumerate([w for w in order if w[0] in MISC])}

        def in_order(table):
            for w in order:
                if w[0] in table:
                    table[w[0]](*w[1:])

        x_v = x.rearrange("b (t p) d -> p b t d", p=P)
        out_v = out.rearrange("b (t p) d -> p (b t) d", p=P)
        block = ctx.enter_context(nc.Block())

        @block.sync
        def _(sp):
            for b in range(B):
                sp.dma_start(xt[:, TILES * b:TILES * (b + 1), :], x_v[:, b]).then_inc(s_x[b], 16)
            sp.dma_start(w12[:, :, :], w12_t).then_inc(s_wf, 16)
            sp.dma_start(w3[:, :, :, :], w3_t).then_inc(s_wf, 16)
            sp.wait_ge(s_zero, 1)
            for n in range(0, NBLK, 8):
                m = min(8, NBLK - n)
                sp.dma_start(xs_dram[n * P:(n + m) * P, :].rearrange("(p r) d -> p (r d)", p=P),
                             zeros[:, 0:m * D]).then_inc(s_xz, 16)

            def bounce(b):
                sp.wait_ge(s_rest, 2 * b + 2)
                sp.dma_start(qk_dram[b], parts[:, b % 2]).then_inc(s_bounce[b], 16)

            def quad_in(s):
                b, g = s // QUADS, s % QUADS
                if s >= QUADS:
                    sp.wait_ge(s_st, NEXP * (s - QUADS + 1))
                if g == 0:
                    sp.wait_ge(s_bounce[b], 16)
                if s == 0:
                    sp.wait_ge(s_kxz, 2)
                if s >= QUADS:
                    sp.dma_start(qx[SHIFT_ROW:SHIFT_ROW + SHIFT_PARTS, g].rearrange("p c t -> p (c t)"),
                                 zeros[0:SHIFT_PARTS, :].bitcast(BF16)).then_inc(s_slot[g], 16)
                src = qk_dram[b].rearrange("(h d) w a t -> w a d h t", d=DK)
                hs = slice(QUAD * g, QUAD * (g + 1))
                for n in range(len(Q_PART)):
                    rows = slice(DK * n, DK * (n + 1))
                    sp.dma_start(qx[rows, g], src[0, Q_PART[n], :, hs]).then_inc(s_slot[g], 16)
                    sp.dma_start(kx[rows, g], src[1, K_PART[n], :, hs]).then_inc(s_slot[g], 16)

            def shift(s):
                g = s % QUADS
                sp.wait_ge(s_nm, s + 1)
                for a in range(SHIFT_PARTS):
                    sp.dma_start(qx[SHIFT_ROW + a:SHIFT_ROW + a + 1, g].rearrange("p c (i j) -> p (c i) j", j=P),
                                 nm_parts[:, s % 2, a, :]).then_inc(s_shift[g], 16)

            def block_in(n):
                if n == 0:
                    sp.wait_ge(s_xs_out, 16 * NT * TOP)
                if n >= NXS:
                    sp.wait_ge(s_f1, n - NXS + 1)
                sp.dma_start(xs[:, n % NXS, :], xs_dram[n * P:(n + 1) * P, :]).then_inc(s_xs[n % NXS], 16)

            def ffn(u):
                if u == 0:
                    for n in range(NXS - 1):
                        block_in(n)
                if u + NXS - 1 < NBLK:
                    block_in(u + NXS - 1)
                if u >= 3:
                    sp.wait_ge(s_fx, u + 1)
                    sp.dma_start(ys_dram[(u - 3) * P:(u - 2) * P, :], fx[:, u % 3, 384:512]).then_inc(s_ys[u % 3], 16)

            def parts_out(b):
                bounce(b)
                if b == 0:
                    for s in range(QUADS):
                        quad_in(s)

            def shift_and_next(s):
                shift(s)
                if s >= 1 and s + QUADS - 1 < STEPS:
                    quad_in(s + QUADS - 1)

            in_order({"k": parts_out, "shift": shift_and_next, "ffn": ffn})
            for t in range(NT):
                sp.wait_ge(s_res, t + 1)
                sp.dma_start(out_v[:, t, :], xt[:, t, :]).then_inc(s_out, 16)
            sp.wait_ge(s_out, 16 * NT)

        @block.gpsimd
        def _(pool):
            n_chain = [0]

            def link(ins):
                n_chain[0] += 1
                ins.then_inc(s_pc, 1)
                pool.wait_ge(s_pc, n_chain[0])

            g = nc.gpsimd
            link(g.memset(ident[:], 0.0))
            g.affine_select(out=ident[:], in_=ident[:], compare_op=ALU.not_equal, fill=1.0, base=0,
                            pattern=[[-1, P]], channel_multiplier=1).then_inc(s_const, 1)

            def normalize(b):
                pool.wait_ge(s_x[b], 16)
                pool.wait_ge(s_rstd, b + 1)
                for t in range(TILES * b, TILES * (b + 1)):
                    ins = g.tensor_scalar(xn[:, t, :], xt[:, t, :], rstd[:, t:t + 1], nmr[:, t:t + 1], ALU.mult, ALU.add)
                ins.then_inc(s_xn, 1)

            normalize(0)
            pool.wait_ge(s_const, 1)
            g.tensor_copy(ident_bf[:], ident[:]).then_inc(s_const, 1)
            link(g.memset(future[:], 0.0))
            g.affine_select(out=future[:], in_=future[:], compare_op=ALU.is_ge, fill=MASKED, base=0,
                            pattern=[[-1, P]], channel_multiplier=1).then_inc(s_const, 1)

            def rest_of(b):
                pool.wait_ge(s_part, 2 * b + 1)
                if b:
                    pool.wait_ge(s_rest, 2 * b)
                g.tensor_tensor(rest[:, :, :], qkf[:, b % 2], parts[:, b % 2, :, 0, :], ALU.subtract).then_inc(s_rest, 1)
                pool.wait_ge(s_part, 2 * b + 2)
                g.tensor_tensor(parts[:, b % 2, :, 2, :], rest[:, :, :], parts[:, b % 2, :, 1, :],
                                ALU.subtract).then_inc(s_rest, 1)

            for b in range(1, B):
                normalize(b)
            g.memset(v[:].rearrange("p a b c d -> p (a b c) d")[:, :, DK + 1:VW], 0.0)
            g.memset(v[:].rearrange("p a b c d -> p (a b c) d")[:, :, DK:DK + 1], 1.0).then_inc(s_v1, 1)
            link(g.memset(before[:], 1.0))
            g.affine_select(out=before[:], in_=before[:], compare_op=ALU.is_gt, fill=0.0, base=0,
                            pattern=[[1, P]], channel_multiplier=-1).then_inc(s_const, 1)
            g.iota(iota_e[:], [[1, EXPERTS]], base=0, channel_multiplier=0, allow_small_or_imprecise_dtypes=True)
            g.iota(iota_128[:], [[P, NT]], base=0, channel_multiplier=0, allow_small_or_imprecise_dtypes=True)
            g.iota(iota_blk[:], [[1, NBLK]], base=0, channel_multiplier=0, allow_small_or_imprecise_dtypes=True)
            link(g.memset(tri_e[:], 1.0))
            g.affine_select(out=tri_e[:], in_=tri_e[:], compare_op=ALU.is_gt, fill=0.0, base=0,
                            pattern=[[1, EXPERTS], [-1, EXPERTS]], channel_multiplier=0).then_inc(s_const, 1)

            def causal(s):
                for pair in range(2):
                    pool.wait_ge(s_exp, NEXP * s + 5 * (pair + 1))
                    for at, stride, n in DIAGONALS:
                        o = 2560 * pair + at
                        if n == 1:
                            view = probs[:, s % 2, o:o + P]
                            pattern = [[1, P]]
                        else:
                            base = 2560 * pair + at - (at % 512)
                            view = probs[:, s % 2, base:base + 512 * n].rearrange("p (a b) -> p a b", b=512)[:, :, at % 512:at % 512 + P]
                            pattern = [[0, n], [1, P]]
                        ins = g.affine_select(out=view, in_=view, compare_op=ALU.is_ge, fill=0.0, base=0,
                                              pattern=pattern, channel_multiplier=-1)
                    ins.then_inc(s_sel, 1)

            def shift(s):
                r, q = nmr_rows[:, s % 2, :], nm_parts[:, s % 2]
                e = nm_rest[:, s % 2, :]
                pool.wait_ge(s_mf, turn["shift", s] + 1)
                if s >= 2:
                    pool.wait_ge(s_shift[s % QUADS - 2 if s % QUADS >= 2 else s % QUADS + 2], 48 * ((s - 2) // QUADS + 1))
                link(g.tensor_scalar(q[:, 0, :], r, 1.0, 0.0, ALU.mult, ALU.add))
                link(g.tensor_tensor(e, r, q[:, 0, :], ALU.subtract))
                link(g.tensor_scalar(q[:, 1, :], e, 1.0, 0.0, ALU.mult, ALU.add))
                g.tensor_tensor(q[:, 2, :], e, q[:, 1, :], ALU.subtract).then_inc(s_nm, 1)

            def scatter(n0, n1):
                if n0 == 0:
                    pool.wait_ge(s_pos, 1)
                    pool.wait_ge(s_xz, 16 * ((NBLK + 7) // 8))
                    pool.wait_ge(s_xn, B)
                for n in range(n0, n1):
                    g.indirect_dma_start(out=xs_dram[:, :], out_offset=bass.IndirectOffsetOnAxis(ap=pos[:, n:n + 1], axis=0),
                                         in_=xn[:, n // TOP, :], in_offset=None).then_inc(s_xs_out, 16)

            def exp1(s, k):
                if k == NEXP - 1:
                    causal(s)
                    if s in (2, 3):
                        scatter(16 * (s - 2), 16 * (s - 1))

            in_order({"exp1": exp1, "shift": shift, "k": rest_of})

            def gather(t):
                if t == 0:
                    for i in range(3):
                        n = len([u for u in range(3, UNITS) if u % 3 == i])
                        pool.wait_ge(s_ys[i], 16 * n)
                if t >= 4:
                    pool.wait_ge(s_res, t - 3)
                for c in range(TOP):
                    g.indirect_dma_start(out=yg[:, t % 4, c, :], out_offset=None, in_=ys_dram[:, :],
                                         in_offset=bass.IndirectOffsetOnAxis(ap=pos[:, TOP * t + c:TOP * t + c + 1], axis=0)
                                         ).then_inc(s_yg[t % 4], 16)

            for t in range(NT):
                gather(t)

        @block.scalar
        def _(act):
            a = nc.scalar
            act.dma_start(wqkv[:, :], w_qkv).then_inc(s_w, 16)
            act.dma_start(bq[:, :], bqk_t).then_inc(s_w, 16)
            act.dma_start(wvg[:, D:D + EXPERTS], wg_t).then_inc(s_w, 16)
            act.dma_start(bv_row[:, :], b_qkv[2 * D:3 * D].rearrange("(a d) -> a d", a=1).to_broadcast([P, D])).then_inc(s_w, 16)
            act.dma_start(bo_row[:, :], b_o.rearrange("(a d) -> a d", a=1).to_broadcast([P, D])).then_inc(s_w, 16)
            act.dma_start(wo[:, :], w_o).then_inc(s_w, 16)
            for b in range(B):
                act.wait_ge(s_ve, b + 1)
                a.activation(sd[:, TILES * b:TILES * (b + 1)], ve[:, TILES * b:TILES * (b + 1)], ACT.Sqrt).then_inc(s_sd, 1)

            def xnT_read(b):
                act.wait_ge(s_m, turn["xnT", b] + 1)
                a.copy(xnT[:, b, :], M[:, :]).then_inc(s_mf, 1)

            def k_parts(b):
                act.wait_ge(s_mf, turn["k", b] + 1)
                if b >= 2:
                    act.wait_ge(s_bounce[b - 2], 16)
                a.copy(parts[:, b % 2, :, 0, :], qkf[:, b % 2]).then_inc(s_part, 1)
                act.wait_ge(s_rest, 2 * b + 1)
                a.copy(parts[:, b % 2, :, 1, :], rest[:, :, :]).then_inc(s_part, 1)

            def exp1(s, k):
                n = NEXP * s + k
                act.wait_ge(s_st, n + 1)
                if s >= 2 and k == 0:
                    act.wait_ge(s_po, s - 1)
                a.activation(probs[:, s % 2, 512 * k:512 * (k + 1)], ST[n % 2][:, :], ACT.Exp).then_inc(s_exp, 1)

            def pv(s):
                act.wait_ge(s_po, s + 1)
                if s >= OTS:
                    act.wait_ge(s_m, turn["otT", (s - OTS) // QUADS, TILES - 1] + 1)
                a.copy(ot[:, s % OTS, :], PO[:, :]).then_inc(s_ot, 1)

            def ffn(u):
                if u == 0:
                    act.wait_ge(s_rest, 2 * B)
                act.wait_ge(s_f1, u + 1)
                if u >= 6:
                    act.wait_ge(s_ys[u % 3], 16 * (u // 3 - 1))
                a.copy(fx[:, u % 3, :], FM[:, :]).then_inc(s_fx, 1)
                if 1 <= u <= NBLK:
                    act.wait_ge(s_fh, u)
                    if u >= 2:
                        act.wait_ge(s_hid, u - 1)
                    a.activation(th[:, :], FH[:, 0:F], ACT.Tanh, scale=0.5).then_inc(s_th, 1)

            def route():
                act.wait_ge(s_ds, 1)
                a.activation(esc[:, :], dsc[:, :], ACT.Exp).then_inc(s_es, 1)

            def onT_read(b):
                act.wait_ge(s_m, turn["onT", b] + 1)
                a.copy(onT[:, :], M[:, :]).then_inc(s_mf, 1)

            in_order({"xnT": xnT_read, "k": k_parts, "exp1": exp1, "pv": pv, "ffn": ffn, "route": route, "onT": onT_read})

        @block.vector
        def _(dve):
            e = nc.vector
            n_chain = [0]

            def link(ins):
                n_chain[0] += 1
                ins.then_inc(s_dc, 1)
                dve.wait_ge(s_dc, n_chain[0])

            e.memset(zeros[:], 0.0).then_inc(s_zero, 1)
            for b in range(B):
                ts = slice(TILES * b, TILES * (b + 1))
                dve.wait_ge(s_x[b], 16)
                for t in range(TILES * b, TILES * (b + 1)):
                    ins = e.bn_stats(stats[:, t, :], xt[:, t, :])
                link(ins)
                for t in range(TILES * b, TILES * (b + 1)):
                    ins = e.bn_aggr(mv[:, t, :], stats[:, t, :])
                link(ins)
                e.tensor_scalar(ve[:, ts], mv[:, ts, 1], EPS, None, ALU.add).then_inc(s_ve, 1)
                dve.wait_ge(s_sd, b + 1)
                link(e.reciprocal(rstd[:, ts], sd[:, ts]))
                e.scalar_tensor_tensor(out=nmr[:, ts], in0=mv[:, ts, 0], scalar=-1.0, in1=rstd[:, ts],
                                       op0=ALU.mult, op1=ALU.mult).then_inc(s_rstd, 1)
                if b == 0:
                    dve.wait_ge(s_w, 16 * 6)
                    e.tensor_copy(wvg[:, 0:D], wqkv[:, 2 * D:3 * D]).then_inc(s_wvg, 1)
                    e.memset(qx[0:ROWS].rearrange("p a b c -> p (a b c)").bitcast(U32), 0).then_inc(s_kxz, 1)
                    link(e.memset(kx[0:ROWS].rearrange("p a b c -> p (a b c)").bitcast(U32), 0))
                    e.memset(kx[SHIFT_ROW:SHIFT_ROW + SHIFT_PARTS].rearrange("p a b c -> p (a b c)"), 1.0).then_inc(s_kxz, 1)
            e.memset(ones_bf[:], 1.0)
            e.memset(PO[:, :], 0.0).then_inc(s_poz, 1)
            e.tensor_tensor(xa[:, :, :], xt[:, :, :], bo_row[:, None, :].to_broadcast([P, NT, D]), ALU.add).then_inc(s_xa, 1)

            def q_read(b):
                dve.wait_ge(s_m, turn["q", b] + 1)
                if b >= 2:
                    dve.wait_ge(s_rest, 2 * b - 3)
                e.tensor_scalar(qkf[:, b % 2, 0, :], M[:, :], bq[:, 0:1], SCALE, ALU.add, ALU.mult).then_inc(s_mf, 1)

            def k_read(b):
                dve.wait_ge(s_m, turn["k", b] + 1)
                e.tensor_scalar(qkf[:, b % 2, 1, :], M[:, :], bq[:, 1:2], None, ALU.add).then_inc(s_mf, 1)

            def v_read(b, half):
                dve.wait_ge(s_m, turn["v", b, half] + 1)
                m = M[:, :].rearrange("p (t c) -> p t c", t=2)
                for i in range(2):
                    t = 2 * half + i
                    e.tensor_tensor(v[:, b, t, :, 0:DK], m[:, i, 0:D].rearrange("p (h d) -> p h d", d=DK),
                                    bv_row[:, :].rearrange("p (h d) -> p h d", d=DK), ALU.add).then_inc(s_v, 1)
                t = TILES * b + 2 * half
                e.tensor_copy(sc[:, t:t + 2, :], m[:, :, D:D + EXPERTS]).then_inc(s_mf, 1)

            def max1(s, k):
                n = NMAX * s + k
                i, c, heads = MAX_GROUPS[k]
                dve.wait_ge(s_sm, n + 1)
                if k == 0 and s >= 2:
                    dve.wait_ge(s_m, turn["shift", s - 2] + 1)
                w = P * (i + 1)
                e.tensor_reduce(nmax[:, s % 2, c:c + heads, i], SM[n % 2][:, 0:heads * w].rearrange("p (c w) -> p c w", w=w),
                                AX.X, ALU.max, negate=True).then_inc(s_max, 1)

            def shift(s):
                dve.wait_ge(s_m, turn["shift", s] + 1)
                if s >= 2:
                    dve.wait_ge(s_nm, s - 1)
                e.tensor_copy(nmr_rows[:, s % 2, :], M[0:TILES * QUAD, 0:P]).then_inc(s_mf, 1)

            def otT(b, i):
                dve.wait_ge(s_m, turn["otT", b, i] + 1)
                m = M[:, :].rearrange("p (h r) -> p h r", r=32)
                link(e.reciprocal(rden[:, :], m[:, :, DK]))
                if b:
                    dve.wait_ge(s_m, turn["onT", b - 1] + 1)
                e.tensor_tensor(on[:, i, :].rearrange("p (h d) -> p h d", d=DK), m[:, :, 0:DK],
                                rden[:, :, None].to_broadcast([P, HEADS, DK]), ALU.mult).then_inc(s_mf, 1)

            def wo_read(b):
                dve.wait_ge(s_m, turn["wo", b] + 1)
                dve.wait_ge(s_xa, 1)
                ts = slice(TILES * b, TILES * (b + 1))
                e.tensor_tensor(xa[:, ts, :], M[:, :].rearrange("p (t d) -> p t d", d=D), xa[:, ts, :], ALU.add).then_inc(s_mf, 1)

            def ffn(u):
                if 1 <= u <= NBLK:
                    n = u - 1
                    dve.wait_ge(s_th, u)
                    link(e.scalar_tensor_tensor(out=th[:, :], in0=th[:, :], scalar=1.0, in1=FH[:, 0:F],
                                                op0=ALU.add, op1=ALU.mult))
                    if n >= 2:
                        dve.wait_ge(s_f1, n + 1)
                    e.scalar_tensor_tensor(out=hid[:, n % 2, :], in0=th[:, :], scalar=0.5, in1=FH[:, F:2 * F],
                                           op0=ALU.mult, op1=ALU.mult).then_inc(s_hid, 1)

            def route():
                dve.wait_ge(s_const, 5)
                dve.wait_ge(s_mf, turn["v", B - 1, 1] + 1)
                for t in range(NT):
                    ins = e.max(mx[:, t, :], sc[:, t, :])
                link(ins)
                e.tensor_tensor(dsc[:, :], mx[:, :, 1], mx[:, :, 0], ALU.subtract).then_inc(s_ds, 1)
                for t in range(NT):
                    ins = e.max_index(ix[:, t, :], mx[:, t, :], sc[:, t, :])
                link(ins)
                link(e.tensor_copy(ixf[:, :, :], ix[:, :, 0:TOP]))
                oh = onehot[:, :, :]
                e.tensor_tensor(oh, ixf[:, :, :].rearrange("p t k -> p (t k)")[:, :, None].to_broadcast([P, NT * TOP, EXPERTS]),
                                iota_e[:, None, :].to_broadcast([P, NT * TOP, EXPERTS]), ALU.is_equal).then_inc(s_oh, 1)
                dve.wait_ge(s_oh, 1)
                with nc.allow_low_precision(reason="counts up to 32 are exact"):
                    e.tensor_reduce(cnt[:, :], oh.rearrange("p n e -> p e n"), AX.X, ALU.add).then_inc(s_oh, 1)
                dve.wait_ge(s_es, 1)
                link(e.tensor_scalar(dsc[:, :], esc[:, :], 1.0, None, ALU.add))
                link(e.reciprocal(prob[:, 0, :], dsc[:, :]))
                e.tensor_tensor(prob[:, 1, :], prob[:, 0, :], esc[:, :], ALU.mult)
                dve.wait_ge(s_rank, 1)
                link(e.tensor_copy(total[:, :], FH[:, NT * TOP * EXPERTS:NT * TOP * EXPERTS + EXPERTS]))
                link(e.tensor_tensor(over[:, :, :], total[:, :, None].to_broadcast([P, EXPERTS, NT]),
                                     iota_128[:, None, :].to_broadcast([P, EXPERTS, NT]), ALU.is_gt))
                link(e.tensor_reduce(nblk[:, :], over[:, :, :], AX.X, ALU.add))
                link(e.tensor_tensor(tri_t[:, :, :], tri_e[:, :, :], nblk[:, None, :].to_broadcast([P, EXPERTS, EXPERTS]), ALU.mult))
                link(e.tensor_reduce(first[:, :], tri_t[:, :, :], AX.X, ALU.add))
                e.tensor_tensor(last[:, :], first[:, :], nblk[:, :], ALU.add)
                link(e.tensor_scalar(first128[:, :], first[:, :], float(P), None, ALU.mult))
                link(e.tensor_tensor(rank[:, :, :], FH[:, 0:NT * TOP * EXPERTS].rearrange("p (n e) -> p n e", e=EXPERTS),
                                     first128[:, None, :].to_broadcast([P, NT * TOP, EXPERTS]), ALU.add))
                link(e.tensor_tensor(rank[:, :, :], rank[:, :, :], oh, ALU.mult))
                link(e.tensor_reduce(posf[:, :], rank[:, :, :], AX.X, ALU.add))
                e.tensor_copy(pos[:, :], posf[:, :]).then_inc(s_pos, 1)
                link(e.tensor_tensor(past[:, :, :], iota_blk[:, :, None].to_broadcast([P, NBLK, EXPERTS]),
                                     last[:, None, :].to_broadcast([P, NBLK, EXPERTS]), ALU.is_ge))
                link(e.tensor_reduce(ebf[:, :], past[:, :, :], AX.X, ALU.add))
                e.tensor_scalar(eb[:, :], ebf[:, :], float(EXPERTS - 1), None, ALU.min).then_inc(s_eb, 1)

            in_order({"q": q_read, "k": k_read, "v": v_read, "max1": max1, "shift": shift, "otT": otT, "wo": wo_read,
                      "ffn": ffn, "route": route})
            for t in range(NT):
                dve.wait_ge(s_yg[t % 4], 16 * TOP * (t // 4 + 1))
                link(e.scalar_tensor_tensor(out=acc[:, t % 4, :], in0=yg[:, t % 4, 0, :], scalar=prob[:, 0, t:t + 1],
                                            in1=xa[:, t, :], op0=ALU.mult, op1=ALU.add))
                e.scalar_tensor_tensor(out=xt[:, t, :], in0=yg[:, t % 4, 1, :], scalar=prob[:, 1, t:t + 1],
                                       in1=acc[:, t % 4, :], op0=ALU.mult, op1=ALU.add).then_inc(s_res, 1)

        @block.tensor
        def _(pe):
            t_ = nc.tensor

            def my_turn(*w):
                if turn[w] > 0:
                    pe.wait_ge(s_mf, turn[w])

            def xnT_(b):
                my_turn("xnT", b)
                if b == 0:
                    pe.wait_ge(s_const, 1)
                pe.wait_ge(s_xn, b + 1)
                for i in range(TILES):
                    ins = t_.transpose(M[:, P * i:P * (i + 1)], xn[:, TILES * b + i, :], ident[:, :])
                ins.then_inc(s_m, 1)

            def q_(b):
                my_turn("q", b)
                if b == 0:
                    pe.wait_ge(s_w, 16 * 6)
                t_.matmul(M[:, :], wqkv[:, 0:D], xnT[:, b, :], start=True, stop=True).then_inc(s_m, 1)

            def k_(b):
                my_turn("k", b)
                t_.matmul(M[:, :], wqkv[:, D:2 * D], xnT[:, b, :], start=True, stop=True).then_inc(s_m, 1)

            def v_(b, half):
                my_turn("v", b, half)
                if b == 0:
                    pe.wait_ge(s_wvg, 1)
                for i in range(2):
                    t = 2 * half + i
                    ins = t_.matmul(M[:, 256 * i:256 * i + D + EXPERTS], xnT[:, b, P * t:P * (t + 1)], wvg[:, :],
                                    start=True, stop=True)
                ins.then_inc(s_m, 1)

            def max1(s, k):
                n = NMAX * s + k
                g = s % QUADS
                if k == 0:
                    pe.wait_ge(s_slot[g], (16 * 12 if s < QUADS else 16 * 12 + 16 * 13 * (s // QUADS)))
                if n == 0:
                    pe.wait_ge(s_const, 3)
                if n >= 2:
                    pe.wait_ge(s_max, n - 1)
                i, c0, heads = MAX_GROUPS[k]
                w = P * (i + 1)
                bank = SM[n % 2]
                for c in range(heads):
                    t_.matmul(bank[:, w * c:w * (c + 1)], qx[0:ROWS, g, c0 + c, P * i:P * (i + 1)],
                              kx[0:ROWS, g, c0 + c, 0:w], start=(c == 0), stop=False, skip_group_check=True)
                for c in range(heads):
                    at = w * c + P * i
                    ins = t_.matmul(bank[:, at:at + P], ident_bf[:, :], future[:, :], start=False, stop=(c == heads - 1),
                                    skip_group_check=True)
                ins.then_inc(s_sm, 1)

            def shift(s):
                my_turn("shift", s)
                pe.wait_ge(s_max, NMAX * (s + 1))
                t_.transpose(M[0:TILES * QUAD, 0:P], nmax[:, s % 2, :, :].rearrange("p c i -> p (c i)"),
                             ident[:, :]).then_inc(s_m, 1)

            def exp1(s, k):
                n = NEXP * s + k
                g = s % QUADS
                if k == 0:
                    pe.wait_ge(s_shift[g], 48 * (s // QUADS + 1))
                if n >= 2:
                    pe.wait_ge(s_exp, n - 1)
                for m, (c, j, at) in enumerate(CHUNKS[k % 5]):
                    h = 2 * (k // 5) + c
                    w = T - P * j
                    ins = t_.matmul(ST[n % 2][:, at:at + w], kx[0:ROWS, g, h, P * j:P * (j + 1)],
                                    qx[0:ROWS, g, h, P * j:T], start=(m == 0), stop=True, skip_group_check=True)
                ins.then_inc(s_st, 1)

            def pv(s):
                b, g = s // QUADS, s % QUADS
                pe.wait_ge(s_sel, 2 * (s + 1))
                if s >= 1:
                    pe.wait_ge(s_ot, s)
                if g == 0:
                    pe.wait_ge(s_v, TILES * (b + 1))
                if s == 0:
                    pe.wait_ge(s_v1, 1)
                    pe.wait_ge(s_poz, 1)
                for j in range(TILES):
                    w = T - P * j
                    for c in range(QUAD):
                        n, at = chunk_of(c, j)
                        o = 512 * n + at
                        ins = t_.matmul(PO[32 * c:32 * c + VW, P * j:T], v[:, b, j, QUAD * g + c, :],
                                        probs[:, s % 2, o:o + w], start=(j == 0), stop=(j == TILES - 1))
                ins.then_inc(s_po, 1)

            def otT(b, i):
                my_turn("otT", b, i)
                pe.wait_ge(s_ot, QUADS * (b + 1))
                for g in range(QUADS):
                    ins = t_.transpose(M[:, P * g:P * (g + 1)], ot[:, (QUADS * b + g) % OTS, P * i:P * (i + 1)], ident[:, :])
                ins.then_inc(s_m, 1)

            def onT_(b):
                my_turn("onT", b)
                for i in range(TILES):
                    ins = t_.transpose(M[:, P * i:P * (i + 1)], on[:, i, :], ident[:, :])
                ins.then_inc(s_m, 1)

            def wo_(b):
                my_turn("wo", b)
                for i in range(TILES):
                    ins = t_.matmul(M[:, D * i:D * (i + 1)], onT[:, P * i:P * (i + 1)], wo[:, :], start=True, stop=True)
                ins.then_inc(s_m, 1)

            def route():
                pe.wait_ge(s_oh, 2)
                N = NT * TOP
                oh = onehot[:, :, :].rearrange("p n e -> p (n e)")
                t_.matmul(FH[:, 0:N * EXPERTS], before[:, :], oh, start=True, stop=False, skip_group_check=True)
                for d in range(1, N):
                    t_.matmul(FH[:, d * EXPERTS:N * EXPERTS], ones_bf[:, :], oh[:, 0:(N - d) * EXPERTS],
                              start=False, stop=(d == N - 1), skip_group_check=True)
                t_.matmul(FH[:, N * EXPERTS:(N + 1) * EXPERTS], ones_bf[:, :], cnt[:, :],
                          start=False, stop=True, skip_group_check=True).then_inc(s_rank, 1)

            def ffn(u):
                if u == 0:
                    pe.wait_ge(s_eb, 1)
                    pe.wait_ge(s_wf, 32)
                if u >= 1:
                    pe.wait_ge(s_fx, u)
                if u < NBLK:
                    pe.wait_ge(s_xs[u % NXS], 16 * (u // NXS + 1))
                src = xs[:, u % NXS, :]
                if u < NBLK:
                    ins = t_.transpose(FM[:, 0:P], src, ident[:, :])
                if 2 <= u < NBLK + 2:
                    pe.wait_ge(s_hid, u - 1)
                    h = hid[:, (u - 2) % 2, :]
                    for c in range(FC):
                        ins = t_.transpose(FM[:, P * (c + 1):P * (c + 2)], h[:, P * c:P * (c + 1)], ident[:, :])
                elif u < 2:
                    for c in range(FC):
                        ins = t_.transpose(FM[:, P * (c + 1):P * (c + 2)], src, ident[:, :])
                if u >= 3:
                    e3 = t_.value_load(eb[0:1, u - 3:u - 2], min_val=0, max_val=EXPERTS - 1)
                    for c in range(FC):
                        ins = t_.matmul(FM[:, 384:512], fx[:, (u - 1) % 3, P * (c + 1):P * (c + 2)],
                                        w3[:, bass.ds(e3, 1), c, :], start=(c == 0), stop=(c == FC - 1), skip_group_check=True)
                else:
                    ins = t_.transpose(FM[:, 384:512], src, ident[:, :])
                ins.then_inc(s_f1, 1)
                if 1 <= u <= NBLK:
                    e1 = t_.value_load(eb[0:1, u - 1:u], min_val=0, max_val=EXPERTS - 1)
                    if u >= 2:
                        pe.wait_ge(s_hid, u - 1)
                    t_.matmul(FH[:, :], fx[:, (u - 1) % 3, 0:P], w12[:, bass.ds(e1, 1), :], start=True, stop=True).then_inc(s_fh, 1)

            in_order({"xnT": xnT_, "q": q_, "k": k_, "v": v_, "max1": max1, "shift": shift, "exp1": exp1, "pv": pv,
                      "otT": otT, "onT": onT_, "wo": wo_, "route": route, "ffn": ffn})


_OUTS = [((4, 512, 128), 'float32')]


def kernel(**inputs):
    import numpy as _np
    import concourse.bacc as _bacc
    from concourse import mybir as _mybir
    from concourse.bass_utils import run_bass_kernel_spmd as _run

    a = {k: _np.asarray(t) for k, t in inputs.items()}
    E, F, D = a['L0_ffn_W1'].shape
    w12 = _np.concatenate([a['L0_ffn_W1'], a['L0_ffn_W2']], axis=1).transpose(2, 0, 1)
    w3 = a['L0_ffn_W3'].transpose(2, 0, 1).reshape(F // 128, 128, E, D).transpose(1, 2, 0, 3)
    laid = {
        'x': a['L0_attn_x'], 'w_qkv': a['L0_attn_W_qkv'], 'b_qkv': a['L0_attn_b_qkv'],
        'bqk_t': a['L0_attn_b_qkv'][:2 * D].reshape(2, D).T, 'w_o': a['L0_attn_W_o'],
        'b_o': a['L0_attn_b_o'], 'wg_t': a['L0_ffn_Wg'].T, 'w12_t': w12, 'w3_t': w3,
    }
    nc = _bacc.Bacc("TRN2", target_bir_lowering=False, num_devices=1)
    arrays, args = {}, []
    for name, t in laid.items():
        t = _np.ascontiguousarray(t)
        arrays[f"in_{name}_dram"] = t
        args.append(nc.dram_tensor(f"in_{name}_dram", t.shape, _mybir.dt.from_np(t.dtype), kind="ExternalInput").ap())
    for i, (shape, dtype) in enumerate(_OUTS):
        dt = _mybir.dt.from_np(_np.dtype(dtype))
        args.append(nc.dram_tensor(f"out_{i}_dram", shape, dt, kind="ExternalOutput").ap())
    attention_and_experts(nc, *args)
    r = _run(nc, [arrays], core_ids=[0])
    got = tuple(r.results[0][f"out_{i}_dram"] for i in range(len(_OUTS)))
    return got[0]
```

```python
from contextlib import ExitStack

import concourse.bass as bass
from concourse import mybir

ALU = mybir.AluOpType
ACT = mybir.ActivationFunctionType
AX = mybir.AxisListType
F32 = mybir.dt.float32
BF16 = mybir.dt.bfloat16
I32 = mybir.dt.int32
U32 = mybir.dt.uint32

P = 128
HEADS = 16
DK = 8
QUAD = 4
EXPERTS = 8
TOP = 2
EPS = 1e-5
MASKED = -3.0e38

Q_PART = (0, 0, 0, 1, 1, 2)
K_PART = (0, 1, 2, 0, 1, 0)
TERM_ROWS = len(Q_PART) * DK
SHIFT_ROW = 64
SHIFT_PARTS = 3
VW = 16
ROWS = 96

CHUNKS = (((0, 0, 0),), ((1, 0, 0),), ((0, 1, 0), (0, 3, 384)), ((1, 1, 0), (1, 3, 384)), ((0, 2, 0), (1, 2, 256)))
DIAGONALS = ((0, 512, 5), (1408, 512, 2), (2304, 512, 1))
MAX_GROUPS = tuple((3, c, 1) for c in range(4)) + tuple((2, c, 1) for c in range(4)) + ((1, 0, 2), (1, 2, 2), (0, 0, 4))
NMAX = len(MAX_GROUPS)
NEXP = 2 * len(CHUNKS)


def chunk_of(c, j):
    for n, parts in enumerate(CHUNKS):
        for head, tile, col in parts:
            if (head, tile) == (c % 2, j):
                return 5 * (c // 2) + n, col


def attention_and_experts(nc, x, w_qkv, b_qkv, bqk_t, w_o, b_o, wg_t, w12_t, w3_t, out):
    B, T, D = x.shape
    F = w12_t.shape[2] // 2
    TILES = T // P
    NT = B * TILES
    QUADS = HEADS // QUAD
    STEPS = B * QUADS
    FC = F // P
    SLOTS = NT * P * TOP
    NBLK = SLOTS // P + EXPERTS - 1
    SCALE = float(DK) ** -0.5
    FIRST_FFN = 4
    assert D == P and T == 512 and HEADS * DK == D and FC == 2

    with ExitStack() as ctx:
        def sb(name, shape, dt=F32):
            return ctx.enter_context(nc.sbuf_tensor(name, shape, dt))

        def bank(name):
            return ctx.enter_context(nc.psum_tensor(name, [P, 512], F32))

        def sem(name):
            return ctx.enter_context(nc.semaphore(name))

        qk_dram = nc.dram_tensor("qk_parts_dram", [B, P, 2, 3, T], BF16).ap()
        xs_dram = nc.dram_tensor("sorted_x_dram", [NBLK * P, D], F32).ap()
        ys_dram = nc.dram_tensor("sorted_y_dram", [NBLK * P, D], F32).ap()

        OTS = QUADS + 1
        wqkv = sb("wqkv", [P, 3 * D])
        wvg = sb("wvg", [P, D + EXPERTS])
        wo = sb("wo", [P, D])
        w12 = sb("w12", [P, EXPERTS, 2 * F])
        w3 = sb("w3", [P, EXPERTS, FC, D])
        bq = sb("bq", [P, 2])
        bv_row = sb("bv_row", [P, D])
        bo_row = sb("bo_row", [P, D])
        ident = sb("ident", [P, P])
        ident_bf = sb("ident_bf", [P, P], BF16)
        ones_bf = sb("ones_bf", [P, P], BF16)
        before = sb("before", [P, P], BF16)
        future = sb("future", [P, P], BF16)
        iota_e = sb("iota_e", [P, EXPERTS])
        iota_128 = sb("iota_128", [P, NT])
        iota_blk = sb("iota_blk", [P, NBLK])
        tri_e = sb("tri_e", [P, EXPERTS, EXPERTS])
        zeros = sb("zeros", [P, 1024])
        ones_rows = sb("ones_rows", [SHIFT_PARTS, QUAD * T], BF16)
        xt = sb("xt", [P, NT, D])
        xn = sb("xn", [P, NT, D])
        xa = sb("xa", [P, NT, D])
        xnT = sb("xnT", [P, B, T])
        stats = sb("stats", [P, NT, 6])
        mv = sb("mv", [P, NT, 2])
        ve = sb("ve", [P, NT])
        sd = sb("sd", [P, NT])
        rstd = sb("rstd", [P, NT])
        nmr = sb("nmr", [P, NT])
        early = sb("early", [P, 6 * T])
        qkf = early[:, 0:4 * T].rearrange("p (n w t) -> p n w t", n=2, w=2)
        rest = early[:, 4 * T:6 * T].rearrange("p (w t) -> p w t", w=2)
        parts = sb("parts", [P, 2, 2, 3, T], BF16)
        qx = sb("qx", [P, QUADS, QUAD, T], BF16)
        kx = sb("kx", [P, QUADS, QUAD, T], BF16)
        v = sb("v", [P, B, TILES, HEADS, VW])
        nmax = sb("nmax", [P, 2, QUAD, TILES])
        nmr_rows = sb("nmr_rows", [TILES * QUAD, 2, P])
        nm_rest = sb("nm_rest", [TILES * QUAD, 2, P])
        nm_parts = sb("nm_parts", [TILES * QUAD, 2, 3, P], BF16)
        probs = sb("probs", [P, 2, NEXP * 512])
        ot = sb("ot", [P, OTS, T])
        rden = sb("rden", [P, HEADS])
        on = xnT[:, 0, :].rearrange("p (i d) -> p i d", i=TILES)
        onT = xnT[:, 1, :]
        sc = sb("sc", [P, NT, EXPERTS])
        mx = sb("mx", [P, NT, 8])
        ix = sb("ix", [P, NT, 8], U32)
        ixf = sb("ixf", [P, NT, TOP])
        onehot = sb("onehot", [P, NT * TOP, EXPERTS], BF16)
        dsc = sb("dsc", [P, NT])
        esc = sb("esc", [P, NT])
        prob = sb("prob", [P, TOP, NT])
        cnt = sb("cnt", [P, EXPERTS], BF16)
        total = sb("total", [P, EXPERTS])
        over = probs[:, 1, 0:EXPERTS * NT].rearrange("p (e t) -> p e t", t=NT)
        rank = probs[:, 1, 512:512 + NT * TOP * EXPERTS].rearrange("p (n e) -> p n e", e=EXPERTS)
        past = probs[:, 1, 1024:1024 + NBLK * EXPERTS].rearrange("p (n e) -> p n e", e=EXPERTS)
        nblk = sb("nblk", [P, EXPERTS])
        first = sb("first", [P, EXPERTS])
        last = sb("last", [P, EXPERTS])
        first128 = sb("first128", [P, EXPERTS])
        tri_t = sb("tri_t", [P, EXPERTS, EXPERTS])
        posf = sb("posf", [P, NT * TOP])
        pos = sb("pos", [P, NT * TOP], U32)
        ebf = sb("ebf", [P, NBLK])
        eb = sb("eb", [P, NBLK], I32)
        NXS = 4
        xs = sb("xs", [P, NXS, D])
        fx = early[:, 0:3 * 512].rearrange("p (n f) -> p n f", n=3)
        th = sb("th", [P, F])
        hid = sb("hid", [P, 3, F])
        yg = w12[:, :, :].rearrange("p e (n d) -> p (e n) d", d=D)
        acc = early[:, 5 * 512:6 * 512].rearrange("p (n d) -> p n d", n=4)

        SM = [bank(f"SM{i}") for i in range(2)]
        ST = [bank(f"ST{i}") for i in range(2)]
        PO = bank("PO")
        M = bank("M")
        FH = bank("FH")
        FM = bank("FM")

        s_x = [sem(f"x_in{b}") for b in range(B)]
        s_w = sem("w_in")
        s_wf = sem("ffn_w_in")
        s_const = sem("const_done")
        s_pc = sem("pool_chain")
        s_zero = sem("zeros_done")
        s_wvg = sem("wvg_done")
        s_dc = sem("dve_chain")
        s_ve = sem("var_done")
        s_sd = sem("sd_done")
        s_rstd = sem("rstd_done")
        s_xn = sem("xn_done")
        s_acc = sem("last_batch_experts_added")
        s_m = sem("misc_written")
        s_mf = sem("misc_read")
        s_part = sem("parts_done")
        s_rest = sem("rest_done")
        s_bounce = [sem(f"parts_in_dram{b}") for b in range(B)]
        s_slot = [sem(f"qkx_in{g}") for g in range(QUADS)]
        s_shift = [sem(f"shift_in{g}") for g in range(QUADS)]
        s_fill = [sem(f"qkx_filled{g}") for g in range(QUADS)]
        s_v = sem("v_done")
        s_v1 = sem("v_ones_done")
        s_sm = sem("scores_written")
        s_max = sem("max_done")
        s_nm = sem("negmax_parts")
        s_st = sem("scoresT_written")
        s_exp = sem("exp_done")
        s_sel = sem("causal_done")
        s_po = sem("pv_written")
        s_poz = sem("pv_cleared")
        s_ot = sem("pv_read")
        s_oh = sem("onehot_done")
        s_ds = sem("score_gap_done")
        s_es = sem("score_gap_exp")
        s_rank = sem("rank_written")
        s_pos = sem("pos_done")
        s_eb = sem("block_expert_done")
        s_xz = sem("sorted_x_cleared")
        s_xs_out = sem("sorted_x_out")
        s_xs = [sem(f"block_in{i}") for i in range(NXS)]
        s_f1 = sem("ffn_mid_written")
        s_fx = sem("ffn_mid_read")
        s_fh = sem("h_written")
        s_th = sem("tanh_done")
        s_hid = sem("hidden_done")
        s_ys = [sem(f"y_out{i}") for i in range(3)]
        s_yg = [sem(f"y_in{t}") for t in range(NT)]
        s_res = sem("result_done")
        s_out = sem("out_written")

        UNITS = NBLK + 4
        AHEAD = 2
        beside = {(s, k): [] for s in range(STEPS + 3) for k in range(NMAX)}

        def put(at, *work):
            beside[at // NMAX, at % NMAX].append(work)

        for s in range(STEPS):
            if s + AHEAD < STEPS:
                put(NMAX * s + 10, "shift", s + AHEAD)
            put(NMAX * (s + 1) + 4, "pv", s)
        for b in range(B - 1):
            at = NMAX * (QUADS * (b + 1) + 1)
            for i in range(TILES):
                put(at + 1 + 2 * i, "otT", b, i)
            put(at + 9, "onT", b)
            put(at + 10, "wo", b)
        for n in range(NT * TOP):
            put(1 + n, "scatter", n)
        for u in range(UNITS):
            put(NMAX * (FIRST_FFN + u // 5) + (0, 2, 4, 6, 8)[u % 5], "ffn", u)
        done = NMAX * (FIRST_FFN + UNITS // 5 + 1)
        for t in range(NT):
            put(done + 2 * t, "gather", t)
            put(done + 2 * t + 5, "combine", t)
        order = []
        for b in range(B):
            order += [("ln", b), ("xnT", b), ("q", b), ("k", b), ("v", b, 0), ("v", b, 1)]
        order.append(("route",))
        for s in range(AHEAD):
            order += [("max1", s, k) for k in range(NMAX)] + [("shift", s)]
        for s in range(STEPS + 3):
            for k in range(NMAX):
                if s + AHEAD < STEPS:
                    order.append(("max1", s + AHEAD, k))
                if s < STEPS and k < NEXP:
                    order.append(("exp1", s, k))
                order += beside[s, k]
        order += [("otT", B - 1, i) for i in range(TILES)] + [("onT", B - 1), ("wo", B - 1)]
        MISC = ("xnT", "q", "k", "v", "shift", "otT", "onT", "wo")
        turn = {w: n for n, w in enumerate([w for w in order if w[0] in MISC])}

        def in_order(table):
            for w in order:
                if w[0] in table:
                    table[w[0]](*w[1:])

        x_v = x.rearrange("b (t p) d -> p b t d", p=P)
        out_v = out.rearrange("b (t p) d -> p (b t) d", p=P)
        block = ctx.enter_context(nc.Block())

        @block.sync
        def _(sp):
            for b in range(B):
                sp.dma_start(xt[:, TILES * b:TILES * (b + 1), :], x_v[:, b]).then_inc(s_x[b], 16)
            sp.dma_start(w12[:, :, :], w12_t).then_inc(s_wf, 16)
            sp.dma_start(w3[:, :, :, :], w3_t).then_inc(s_wf, 16)
            sp.wait_ge(s_zero, 1)
            for n in range(0, NBLK, 8):
                m = min(8, NBLK - n)
                sp.dma_start(xs_dram[n * P:(n + m) * P, :].rearrange("(p r) d -> p (r d)", p=P),
                             zeros[:, 0:m * D]).then_inc(s_xz, 16)

            def bounce(b):
                sp.wait_ge(s_rest, 2 * b + 2)
                sp.dma_start(qk_dram[b], parts[:, b % 2]).then_inc(s_bounce[b], 16)

            def quad_in(s):
                b, g = s // QUADS, s % QUADS
                if s >= QUADS:
                    sp.wait_ge(s_st, NEXP * (s - QUADS + 1))
                if g == 0:
                    sp.wait_ge(s_bounce[b], 16)
                if s >= QUADS:
                    sp.dma_start(qx[SHIFT_ROW:SHIFT_ROW + SHIFT_PARTS, g].rearrange("p c t -> p (c t)"),
                                 zeros[0:SHIFT_PARTS, :].bitcast(BF16)).then_inc(s_slot[g], 16)
                src = qk_dram[b].rearrange("(h d) w a t -> w a d h t", d=DK)
                hs = slice(QUAD * g, QUAD * (g + 1))
                for n in range(len(Q_PART)):
                    rows = slice(DK * n, DK * (n + 1))
                    sp.dma_start(qx[rows, g], src[0, Q_PART[n], :, hs]).then_inc(s_slot[g], 16)
                    sp.dma_start(kx[rows, g], src[1, K_PART[n], :, hs]).then_inc(s_slot[g], 16)

            def shift(s):
                g = s % QUADS
                sp.wait_ge(s_nm, s + 1)
                for a in range(SHIFT_PARTS):
                    sp.dma_start(qx[SHIFT_ROW + a:SHIFT_ROW + a + 1, g].rearrange("p c (i j) -> p (c i) j", j=P),
                                 nm_parts[:, s % 2, a, :]).then_inc(s_shift[g], 16)

            def block_in(n):
                if n == 0:
                    sp.wait_ge(s_xs_out, 16 * NT * TOP)
                if n >= NXS:
                    sp.wait_ge(s_f1, n - NXS + 1)
                sp.dma_start(xs[:, n % NXS, :], xs_dram[n * P:(n + 1) * P, :]).then_inc(s_xs[n % NXS], 16)

            def ffn(u):
                if u == 0:
                    for n in range(NXS - 1):
                        block_in(n)
                if u + NXS - 1 < NBLK:
                    block_in(u + NXS - 1)
                if u >= 4:
                    sp.wait_ge(s_fx, u + 1)
                    sp.dma_start(ys_dram[(u - 4) * P:(u - 3) * P, :], fx[:, u % 3, 384:512]).then_inc(s_ys[u % 3], 16)

            def parts_out(b):
                bounce(b)
                if b == 0:
                    for s in range(QUADS):
                        quad_in(s)

            def exp1(s, k):
                if k == 2 and s >= 1 and s + QUADS - 1 < STEPS:
                    quad_in(s + QUADS - 1)

            def rows_out(b):
                sp.wait_ge(s_res, TILES * (b + 1) if b < B - 1 else TILES * (B - 1) + 1)
                ts = slice(TILES * b, TILES * (b + 1))
                sp.dma_start(out_v[:, ts, :], xt[:, ts, :]).then_inc(s_out, 16)

            def combine(t):
                if t % TILES == TILES - 1 and t < NT - TILES:
                    rows_out(t // TILES)

            in_order({"k": parts_out, "shift": shift, "exp1": exp1, "ffn": ffn, "combine": combine})
            rows_out(B - 1)
            sp.wait_ge(s_out, 16 * B)

        @block.gpsimd
        def _(pool):
            n_chain = [0]

            def link(ins):
                n_chain[0] += 1
                ins.then_inc(s_pc, 1)
                pool.wait_ge(s_pc, n_chain[0])

            g = nc.gpsimd
            link(g.memset(ident[:], 0.0))
            g.affine_select(out=ident[:], in_=ident[:], compare_op=ALU.not_equal, fill=1.0, base=0,
                            pattern=[[-1, P]], channel_multiplier=1).then_inc(s_const, 1)

            def normalize(b):
                pool.wait_ge(s_x[b], 16)
                pool.wait_ge(s_rstd, b + 1)
                for t in range(TILES * b, TILES * (b + 1)):
                    ins = g.tensor_scalar(xn[:, t, :], xt[:, t, :], rstd[:, t:t + 1], nmr[:, t:t + 1], ALU.mult, ALU.add)
                ins.then_inc(s_xn, 1)

            pool.wait_ge(s_const, 1)
            g.tensor_copy(ident_bf[:], ident[:]).then_inc(s_const, 1)
            link(g.memset(future[:], 0.0))
            g.affine_select(out=future[:], in_=future[:], compare_op=ALU.is_ge, fill=MASKED, base=0,
                            pattern=[[-1, P]], channel_multiplier=1).then_inc(s_const, 1)

            def rest_of(b):
                pool.wait_ge(s_part, 2 * b + 1)
                if b:
                    pool.wait_ge(s_rest, 2 * b)
                g.tensor_tensor(rest[:, :, :], qkf[:, b % 2], parts[:, b % 2, :, 0, :], ALU.subtract).then_inc(s_rest, 1)
                pool.wait_ge(s_part, 2 * b + 2)
                g.tensor_tensor(parts[:, b % 2, :, 2, :], rest[:, :, :], parts[:, b % 2, :, 1, :],
                                ALU.subtract).then_inc(s_rest, 1)

            g.memset(v[:].rearrange("p a b c d -> p (a b c) d")[:, :, DK + 1:VW], 0.0)
            g.memset(v[:].rearrange("p a b c d -> p (a b c) d")[:, :, DK:DK + 1], 1.0).then_inc(s_v1, 1)
            link(g.memset(before[:], 1.0))
            g.affine_select(out=before[:], in_=before[:], compare_op=ALU.is_gt, fill=0.0, base=0,
                            pattern=[[1, P]], channel_multiplier=-1).then_inc(s_const, 1)
            g.iota(iota_e[:], [[1, EXPERTS]], base=0, channel_multiplier=0, allow_small_or_imprecise_dtypes=True)
            g.iota(iota_128[:], [[P, NT]], base=0, channel_multiplier=0, allow_small_or_imprecise_dtypes=True)
            g.iota(iota_blk[:], [[1, NBLK]], base=0, channel_multiplier=0, allow_small_or_imprecise_dtypes=True)
            link(g.memset(tri_e[:], 1.0))
            g.affine_select(out=tri_e[:], in_=tri_e[:], compare_op=ALU.is_gt, fill=0.0, base=0,
                            pattern=[[1, EXPERTS], [-1, EXPERTS]], channel_multiplier=0).then_inc(s_const, 1)

            def causal(s, pair):
                pool.wait_ge(s_exp, NEXP * s + 5 * (pair + 1))
                for at, _, n in DIAGONALS:
                    base = 2560 * pair + at - at % 512
                    view = probs[:, s % 2, base:base + 512 * n].rearrange("p (a b) -> p a b", b=512)[:, :, at % 512:at % 512 + P]
                    ins = g.affine_select(out=view, in_=view, compare_op=ALU.is_ge, fill=0.0, base=0,
                                          pattern=[[0, n], [1, P]], channel_multiplier=-1)
                ins.then_inc(s_sel, 1)

            def shift(s):
                r, q = nmr_rows[:, s % 2, :], nm_parts[:, s % 2]
                e = nm_rest[:, s % 2, :]
                pool.wait_ge(s_mf, turn["shift", s] + 1)
                if s >= 2:
                    pool.wait_ge(s_shift[s % QUADS - 2 if s % QUADS >= 2 else s % QUADS + 2], 48 * ((s - 2) // QUADS + 1))
                link(g.tensor_scalar(q[:, 0, :], r, 1.0, 0.0, ALU.mult, ALU.add))
                link(g.tensor_tensor(e, r, q[:, 0, :], ALU.subtract))
                link(g.tensor_scalar(q[:, 1, :], e, 1.0, 0.0, ALU.mult, ALU.add))
                g.tensor_tensor(q[:, 2, :], e, q[:, 1, :], ALU.subtract).then_inc(s_nm, 1)

            def scatter(n):
                if n == 0:
                    pool.wait_ge(s_pos, 1)
                    pool.wait_ge(s_xz, 16 * ((NBLK + 7) // 8))
                    pool.wait_ge(s_xn, B)
                g.indirect_dma_start(out=xs_dram[:, :], out_offset=bass.IndirectOffsetOnAxis(ap=pos[:, n:n + 1], axis=0),
                                     in_=xn[:, n // TOP, :], in_offset=None).then_inc(s_xs_out, 16)

            def exp1(s, k):
                if k % 5 == 4:
                    causal(s, k // 5)

            def gather(t):
                if t == 0:
                    for i in range(3):
                        pool.wait_ge(s_ys[i], 16 * len([u for u in range(4, UNITS) if u % 3 == i]))
                for c in range(TOP):
                    n = TOP * t + c
                    g.indirect_dma_start(out=yg[:, n, :], out_offset=None, in_=ys_dram[:, :],
                                         in_offset=bass.IndirectOffsetOnAxis(ap=pos[:, n:n + 1], axis=0)
                                         ).then_inc(s_yg[t], 16)

            in_order({"ln": normalize, "exp1": exp1, "shift": shift, "k": rest_of, "scatter": scatter, "gather": gather})

        @block.scalar
        def _(act):
            a = nc.scalar
            act.dma_start(wqkv[:, :], w_qkv).then_inc(s_w, 16)
            act.dma_start(bq[:, :], bqk_t).then_inc(s_w, 16)
            act.dma_start(wvg[:, D:D + EXPERTS], wg_t).then_inc(s_w, 16)
            act.dma_start(bv_row[:, :], b_qkv[2 * D:3 * D].rearrange("(a d) -> a d", a=1).to_broadcast([P, D])).then_inc(s_w, 16)
            act.dma_start(bo_row[:, :], b_o.rearrange("(a d) -> a d", a=1).to_broadcast([P, D])).then_inc(s_w, 16)
            act.dma_start(wo[:, :], w_o).then_inc(s_w, 16)
            act.wait_ge(s_zero, 2)
            zero_bf = zeros[:, :].bitcast(BF16)
            for g in range(QUADS):
                act.dma_start(qx[TERM_ROWS:ROWS, g], zero_bf[TERM_ROWS:ROWS, :]).then_inc(s_fill[g], 16)
                act.dma_start(kx[TERM_ROWS:SHIFT_ROW, g], zero_bf[TERM_ROWS:SHIFT_ROW, :]).then_inc(s_fill[g], 16)
                act.dma_start(kx[SHIFT_ROW + SHIFT_PARTS:ROWS, g], zero_bf[SHIFT_ROW + SHIFT_PARTS:ROWS, :]).then_inc(s_fill[g], 16)
                act.dma_start(kx[SHIFT_ROW:SHIFT_ROW + SHIFT_PARTS, g], ones_rows[:, :]).then_inc(s_fill[g], 16)

            def root(b):
                act.wait_ge(s_ve, b + 1)
                a.activation(sd[:, TILES * b:TILES * (b + 1)], ve[:, TILES * b:TILES * (b + 1)], ACT.Sqrt).then_inc(s_sd, 1)

            def xnT_read(b):
                act.wait_ge(s_m, turn["xnT", b] + 1)
                a.copy(xnT[:, b, :], M[:, :]).then_inc(s_mf, 1)

            def k_parts(b):
                act.wait_ge(s_mf, turn["k", b] + 1)
                if b >= 2:
                    act.wait_ge(s_bounce[b - 2], 16)
                a.copy(parts[:, b % 2, :, 0, :], qkf[:, b % 2]).then_inc(s_part, 1)
                act.wait_ge(s_rest, 2 * b + 1)
                a.copy(parts[:, b % 2, :, 1, :], rest[:, :, :]).then_inc(s_part, 1)

            def exp1(s, k):
                n = NEXP * s + k
                act.wait_ge(s_st, n + 1)
                if s >= 2 and k == 0:
                    act.wait_ge(s_po, s - 1)
                a.activation(probs[:, s % 2, 512 * k:512 * (k + 1)], ST[n % 2][:, :], ACT.Exp).then_inc(s_exp, 1)

            def pv(s):
                act.wait_ge(s_po, s + 1)
                if s >= OTS:
                    act.wait_ge(s_m, turn["otT", (s - OTS) // QUADS, TILES - 1] + 1)
                a.copy(ot[:, s % OTS, :], PO[:, :]).then_inc(s_ot, 1)

            def ffn(u):
                if u == 0:
                    act.wait_ge(s_rest, 2 * B)
                act.wait_ge(s_f1, u + 1)
                if u >= 7:
                    act.wait_ge(s_ys[u % 3], 16 * len(range(4 + (u - 4) % 3, u, 3)))
                a.copy(fx[:, u % 3, :], FM[:, :]).then_inc(s_fx, 1)
                if 1 <= u <= NBLK:
                    act.wait_ge(s_fh, u)
                    if u >= 2:
                        act.wait_ge(s_hid, u - 1)
                    a.activation(th[:, :], FH[:, 0:F], ACT.Tanh, scale=0.5).then_inc(s_th, 1)

            def route():
                act.wait_ge(s_ds, 1)
                a.activation(esc[:, :], dsc[:, :], ACT.Exp).then_inc(s_es, 1)

            def onT_read(b):
                act.wait_ge(s_m, turn["onT", b] + 1)
                a.copy(onT[:, :], M[:, :]).then_inc(s_mf, 1)

            in_order({"ln": root, "xnT": xnT_read, "k": k_parts, "exp1": exp1, "pv": pv, "ffn": ffn, "route": route, "onT": onT_read})

        @block.vector
        def _(dve):
            e = nc.vector
            n_chain = [0]

            def link(ins):
                n_chain[0] += 1
                ins.then_inc(s_dc, 1)
                dve.wait_ge(s_dc, n_chain[0])

            e.memset(zeros[:], 0.0).then_inc(s_zero, 1)
            e.memset(ones_rows[:], 1.0).then_inc(s_zero, 1)

            def layer_norm(b):
                ts = slice(TILES * b, TILES * (b + 1))
                dve.wait_ge(s_x[b], 16)
                for t in range(TILES * b, TILES * (b + 1)):
                    ins = e.bn_stats(stats[:, t, :], xt[:, t, :])
                link(ins)
                for t in range(TILES * b, TILES * (b + 1)):
                    ins = e.bn_aggr(mv[:, t, :], stats[:, t, :])
                link(ins)
                e.tensor_scalar(ve[:, ts], mv[:, ts, 1], EPS, None, ALU.add).then_inc(s_ve, 1)
                dve.wait_ge(s_sd, b + 1)
                link(e.reciprocal(rstd[:, ts], sd[:, ts]))
                e.scalar_tensor_tensor(out=nmr[:, ts], in0=mv[:, ts, 0], scalar=-1.0, in1=rstd[:, ts],
                                       op0=ALU.mult, op1=ALU.mult).then_inc(s_rstd, 1)
                if b == 0:
                    dve.wait_ge(s_w, 16 * 6)
                    e.tensor_copy(wvg[:, 0:D], wqkv[:, 2 * D:3 * D]).then_inc(s_wvg, 1)
                    e.memset(ones_bf[:], 1.0)
                    e.memset(PO[:, :], 0.0).then_inc(s_poz, 1)

            def q_read(b):
                dve.wait_ge(s_m, turn["q", b] + 1)
                if b >= 2:
                    dve.wait_ge(s_rest, 2 * b - 3)
                e.tensor_scalar(qkf[:, b % 2, 0, :], M[:, :], bq[:, 0:1], SCALE, ALU.add, ALU.mult).then_inc(s_mf, 1)

            def k_read(b):
                dve.wait_ge(s_m, turn["k", b] + 1)
                e.tensor_scalar(qkf[:, b % 2, 1, :], M[:, :], bq[:, 1:2], None, ALU.add).then_inc(s_mf, 1)

            def v_read(b, half):
                dve.wait_ge(s_m, turn["v", b, half] + 1)
                m = M[:, :].rearrange("p (t c) -> p t c", t=2)
                for i in range(2):
                    t = 2 * half + i
                    e.tensor_tensor(v[:, b, t, :, 0:DK], m[:, i, 0:D].rearrange("p (h d) -> p h d", d=DK),
                                    bv_row[:, :].rearrange("p (h d) -> p h d", d=DK), ALU.add).then_inc(s_v, 1)
                t = TILES * b + 2 * half
                e.tensor_copy(sc[:, t:t + 2, :], m[:, :, D:D + EXPERTS]).then_inc(s_mf, 1)

            def max1(s, k):
                n = NMAX * s + k
                i, c, heads = MAX_GROUPS[k]
                dve.wait_ge(s_sm, n + 1)
                if k == 0 and s >= 2:
                    dve.wait_ge(s_m, turn["shift", s - 2] + 1)
                w = P * (i + 1)
                e.tensor_reduce(nmax[:, s % 2, c:c + heads, i], SM[n % 2][:, 0:heads * w].rearrange("p (c w) -> p c w", w=w),
                                AX.X, ALU.max, negate=True).then_inc(s_max, 1)

            def shift(s):
                dve.wait_ge(s_m, turn["shift", s] + 1)
                if s >= 2:
                    dve.wait_ge(s_nm, s - 1)
                e.tensor_copy(nmr_rows[:, s % 2, :], M[0:TILES * QUAD, 0:P]).then_inc(s_mf, 1)

            def otT(b, i):
                dve.wait_ge(s_m, turn["otT", b, i] + 1)
                m = M[:, :].rearrange("p (h r) -> p h r", r=32)
                link(e.reciprocal(rden[:, :], m[:, :, DK]))
                if b:
                    dve.wait_ge(s_m, turn["onT", b - 1] + 1)
                e.tensor_tensor(on[:, i, :].rearrange("p (h d) -> p h d", d=DK), m[:, :, 0:DK],
                                rden[:, :, None].to_broadcast([P, HEADS, DK]), ALU.mult).then_inc(s_mf, 1)

            def wo_read(b):
                dve.wait_ge(s_m, turn["wo", b] + 1)
                ts = slice(TILES * b, TILES * (b + 1))
                m = M[:, :].rearrange("p (t d) -> p t d", d=D)
                if b == B - 1:
                    dve.wait_ge(s_res, NT - TILES)
                    dve.wait_ge(s_acc, TILES)
                    e.tensor_tensor(xt[:, ts, :], m, xa[:, ts, :], ALU.add).then_inc(s_res, 1)
                else:
                    e.tensor_tensor(xa[:, ts, :], m, xa[:, ts, :], ALU.add).then_inc(s_mf, 1)

            def combine(t):
                dve.wait_ge(s_yg[t], 16 * TOP)
                link(e.scalar_tensor_tensor(out=acc[:, t % 4, :], in0=yg[:, TOP * t, :], scalar=prob[:, 0, t:t + 1],
                                            in1=xa[:, t, :], op0=ALU.mult, op1=ALU.add))
                last_batch = t >= NT - TILES
                e.scalar_tensor_tensor(out=(xa if last_batch else xt)[:, t, :], in0=yg[:, TOP * t + 1, :],
                                       scalar=prob[:, 1, t:t + 1], in1=acc[:, t % 4, :], op0=ALU.mult,
                                       op1=ALU.add).then_inc(s_acc if last_batch else s_res, 1)

            def ffn(u):
                if 1 <= u <= NBLK:
                    n = u - 1
                    dve.wait_ge(s_th, u)
                    link(e.scalar_tensor_tensor(out=th[:, :], in0=th[:, :], scalar=1.0, in1=FH[:, 0:F],
                                                op0=ALU.add, op1=ALU.mult))
                    if n >= 3:
                        dve.wait_ge(s_f1, n + 1)
                    e.scalar_tensor_tensor(out=hid[:, n % 3, :], in0=th[:, :], scalar=0.5, in1=FH[:, F:2 * F],
                                           op0=ALU.mult, op1=ALU.mult).then_inc(s_hid, 1)

            def route():
                dve.wait_ge(s_const, 5)
                dve.wait_ge(s_mf, turn["v", B - 1, 1] + 1)
                e.tensor_tensor(xa[:, :, :], xt[:, :, :], bo_row[:, None, :].to_broadcast([P, NT, D]), ALU.add)
                for t in range(NT):
                    ins = e.max(mx[:, t, :], sc[:, t, :])
                link(ins)
                e.tensor_tensor(dsc[:, :], mx[:, :, 1], mx[:, :, 0], ALU.subtract).then_inc(s_ds, 1)
                for t in range(NT):
                    ins = e.max_index(ix[:, t, :], mx[:, t, :], sc[:, t, :])
                link(ins)
                link(e.tensor_copy(ixf[:, :, :], ix[:, :, 0:TOP]))
                oh = onehot[:, :, :]
                e.tensor_tensor(oh, ixf[:, :, :].rearrange("p t k -> p (t k)")[:, :, None].to_broadcast([P, NT * TOP, EXPERTS]),
                                iota_e[:, None, :].to_broadcast([P, NT * TOP, EXPERTS]), ALU.is_equal).then_inc(s_oh, 1)
                dve.wait_ge(s_oh, 1)
                with nc.allow_low_precision(reason="counts up to 32 are exact"):
                    e.tensor_reduce(cnt[:, :], oh.rearrange("p n e -> p e n"), AX.X, ALU.add).then_inc(s_oh, 1)
                dve.wait_ge(s_es, 1)
                link(e.tensor_scalar(dsc[:, :], esc[:, :], 1.0, None, ALU.add))
                link(e.reciprocal(prob[:, 0, :], dsc[:, :]))
                e.tensor_tensor(prob[:, 1, :], prob[:, 0, :], esc[:, :], ALU.mult)
                dve.wait_ge(s_rank, 1)
                link(e.tensor_copy(total[:, :], FH[:, NT * TOP * EXPERTS:NT * TOP * EXPERTS + EXPERTS]))
                link(e.tensor_tensor(over[:, :, :], total[:, :, None].to_broadcast([P, EXPERTS, NT]),
                                     iota_128[:, None, :].to_broadcast([P, EXPERTS, NT]), ALU.is_gt))
                link(e.tensor_reduce(nblk[:, :], over[:, :, :], AX.X, ALU.add))
                link(e.tensor_tensor(tri_t[:, :, :], tri_e[:, :, :], nblk[:, None, :].to_broadcast([P, EXPERTS, EXPERTS]), ALU.mult))
                link(e.tensor_reduce(first[:, :], tri_t[:, :, :], AX.X, ALU.add))
                e.tensor_tensor(last[:, :], first[:, :], nblk[:, :], ALU.add)
                link(e.tensor_scalar(first128[:, :], first[:, :], float(P), None, ALU.mult))
                link(e.tensor_tensor(rank[:, :, :], FH[:, 0:NT * TOP * EXPERTS].rearrange("p (n e) -> p n e", e=EXPERTS),
                                     first128[:, None, :].to_broadcast([P, NT * TOP, EXPERTS]), ALU.add))
                link(e.tensor_tensor(rank[:, :, :], rank[:, :, :], oh, ALU.mult))
                link(e.tensor_reduce(posf[:, :], rank[:, :, :], AX.X, ALU.add))
                e.tensor_copy(pos[:, :], posf[:, :]).then_inc(s_pos, 1)
                link(e.tensor_tensor(past[:, :, :], iota_blk[:, :, None].to_broadcast([P, NBLK, EXPERTS]),
                                     last[:, None, :].to_broadcast([P, NBLK, EXPERTS]), ALU.is_ge))
                link(e.tensor_reduce(ebf[:, :], past[:, :, :], AX.X, ALU.add))
                e.tensor_scalar(eb[:, :], ebf[:, :], float(EXPERTS - 1), None, ALU.min).then_inc(s_eb, 1)

            in_order({"ln": layer_norm, "combine": combine, "q": q_read, "k": k_read, "v": v_read, "max1": max1, "shift": shift, "otT": otT, "wo": wo_read,
                      "ffn": ffn, "route": route})

        @block.tensor
        def _(pe):
            t_ = nc.tensor

            def my_turn(*w):
                if turn[w] > 0:
                    pe.wait_ge(s_mf, turn[w])

            def xnT_(b):
                my_turn("xnT", b)
                if b == 0:
                    pe.wait_ge(s_const, 1)
                pe.wait_ge(s_xn, b + 1)
                for i in range(TILES):
                    ins = t_.transpose(M[:, P * i:P * (i + 1)], xn[:, TILES * b + i, :], ident[:, :])
                ins.then_inc(s_m, 1)

            def q_(b):
                my_turn("q", b)
                if b == 0:
                    pe.wait_ge(s_w, 16 * 6)
                t_.matmul(M[:, :], wqkv[:, 0:D], xnT[:, b, :], start=True, stop=True).then_inc(s_m, 1)

            def k_(b):
                my_turn("k", b)
                t_.matmul(M[:, :], wqkv[:, D:2 * D], xnT[:, b, :], start=True, stop=True).then_inc(s_m, 1)

            def v_(b, half):
                my_turn("v", b, half)
                if b == 0:
                    pe.wait_ge(s_wvg, 1)
                for i in range(2):
                    t = 2 * half + i
                    ins = t_.matmul(M[:, 256 * i:256 * i + D + EXPERTS], xnT[:, b, P * t:P * (t + 1)], wvg[:, :],
                                    start=True, stop=True)
                ins.then_inc(s_m, 1)

            def max1(s, k):
                n = NMAX * s + k
                g = s % QUADS
                if k == 0:
                    pe.wait_ge(s_slot[g], (16 * 12 if s < QUADS else 16 * 12 + 16 * 13 * (s // QUADS)))
                if k == 0 and s < QUADS:
                    pe.wait_ge(s_fill[g], 64)
                if n == 0:
                    pe.wait_ge(s_const, 3)
                if n >= 2:
                    pe.wait_ge(s_max, n - 1)
                i, c0, heads = MAX_GROUPS[k]
                w = P * (i + 1)
                bank = SM[n % 2]
                for c in range(heads):
                    t_.matmul(bank[:, w * c:w * (c + 1)], qx[0:ROWS, g, c0 + c, P * i:P * (i + 1)],
                              kx[0:ROWS, g, c0 + c, 0:w], start=(c == 0), stop=False, skip_group_check=True)
                for c in range(heads):
                    at = w * c + P * i
                    ins = t_.matmul(bank[:, at:at + P], ident_bf[:, :], future[:, :], start=False, stop=(c == heads - 1),
                                    skip_group_check=True)
                ins.then_inc(s_sm, 1)

            def shift(s):
                my_turn("shift", s)
                pe.wait_ge(s_max, NMAX * (s + 1))
                t_.transpose(M[0:TILES * QUAD, 0:P], nmax[:, s % 2, :, :].rearrange("p c i -> p (c i)"),
                             ident[:, :]).then_inc(s_m, 1)

            def exp1(s, k):
                n = NEXP * s + k
                g = s % QUADS
                if k == 0:
                    pe.wait_ge(s_shift[g], 48 * (s // QUADS + 1))
                if n >= 2:
                    pe.wait_ge(s_exp, n - 1)
                for m, (c, j, at) in enumerate(CHUNKS[k % 5]):
                    h = 2 * (k // 5) + c
                    w = T - P * j
                    ins = t_.matmul(ST[n % 2][:, at:at + w], kx[0:ROWS, g, h, P * j:P * (j + 1)],
                                    qx[0:ROWS, g, h, P * j:T], start=(m == 0), stop=True, skip_group_check=True)
                ins.then_inc(s_st, 1)

            def pv(s):
                b, g = s // QUADS, s % QUADS
                pe.wait_ge(s_sel, 2 * (s + 1))
                if s >= 1:
                    pe.wait_ge(s_ot, s)
                if g == 0:
                    pe.wait_ge(s_v, TILES * (b + 1))
                if s == 0:
                    pe.wait_ge(s_v1, 1)
                    pe.wait_ge(s_poz, 1)
                for j in range(TILES):
                    w = T - P * j
                    for c in range(QUAD):
                        n, at = chunk_of(c, j)
                        o = 512 * n + at
                        ins = t_.matmul(PO[32 * c:32 * c + VW, P * j:T], v[:, b, j, QUAD * g + c, :],
                                        probs[:, s % 2, o:o + w], start=(j == 0), stop=(j == TILES - 1))
                ins.then_inc(s_po, 1)

            def otT(b, i):
                my_turn("otT", b, i)
                pe.wait_ge(s_ot, QUADS * (b + 1))
                for g in range(QUADS):
                    ins = t_.transpose(M[:, P * g:P * (g + 1)], ot[:, (QUADS * b + g) % OTS, P * i:P * (i + 1)], ident[:, :])
                ins.then_inc(s_m, 1)

            def onT_(b):
                my_turn("onT", b)
                for i in range(TILES):
                    ins = t_.transpose(M[:, P * i:P * (i + 1)], on[:, i, :], ident[:, :])
                ins.then_inc(s_m, 1)

            def wo_(b):
                my_turn("wo", b)
                for i in range(TILES):
                    ins = t_.matmul(M[:, D * i:D * (i + 1)], onT[:, P * i:P * (i + 1)], wo[:, :], start=True, stop=True)
                ins.then_inc(s_m, 1)

            def route():
                pe.wait_ge(s_oh, 2)
                N = NT * TOP
                oh = onehot[:, :, :].rearrange("p n e -> p (n e)")
                t_.matmul(FH[:, 0:N * EXPERTS], before[:, :], oh, start=True, stop=False, skip_group_check=True)
                for d in range(1, N):
                    t_.matmul(FH[:, d * EXPERTS:N * EXPERTS], ones_bf[:, :], oh[:, 0:(N - d) * EXPERTS],
                              start=False, stop=(d == N - 1), skip_group_check=True)
                t_.matmul(FH[:, N * EXPERTS:(N + 1) * EXPERTS], ones_bf[:, :], cnt[:, :],
                          start=False, stop=True, skip_group_check=True).then_inc(s_rank, 1)

            expert = {}

            def ffn(u):
                if u == 0:
                    pe.wait_ge(s_eb, 1)
                    pe.wait_ge(s_wf, 32)
                if u >= 1:
                    pe.wait_ge(s_fx, u)
                src = xs[:, u % NXS, :]
                if u < NBLK:
                    pe.wait_ge(s_xs[u % NXS], 16 * (u // NXS + 1))
                    ins = t_.transpose(FM[:, 0:P], src, ident[:, :])
                if 3 <= u < NBLK + 3:
                    pe.wait_ge(s_hid, u - 2)
                    h = hid[:, u % 3, :]
                    for c in range(FC):
                        ins = t_.transpose(FM[:, P * (c + 1):P * (c + 2)], h[:, P * c:P * (c + 1)], ident[:, :])
                elif u < 3:
                    for c in range(FC):
                        ins = t_.transpose(FM[:, P * (c + 1):P * (c + 2)], src, ident[:, :])
                if u >= 4:
                    e3 = expert.pop(u - 4)
                    for c in range(FC):
                        ins = t_.matmul(FM[:, 384:512], fx[:, (u - 1) % 3, P * (c + 1):P * (c + 2)],
                                        w3[:, bass.ds(e3, 1), c, :], start=(c == 0), stop=(c == FC - 1), skip_group_check=True)
                else:
                    ins = t_.transpose(FM[:, 384:512], src, ident[:, :])
                ins.then_inc(s_f1, 1)
                if 1 <= u <= NBLK:
                    if u >= 2:
                        pe.wait_ge(s_hid, u - 1)
                    t_.matmul(FH[:, :], fx[:, (u - 1) % 3, 0:P], w12[:, bass.ds(expert[u - 1], 1), :],
                              start=True, stop=True).then_inc(s_fh, 1)
                if u < NBLK:
                    expert[u] = t_.value_load(eb[0:1, u:u + 1], min_val=0, max_val=EXPERTS - 1)

            in_order({"xnT": xnT_, "q": q_, "k": k_, "v": v_, "max1": max1, "shift": shift, "exp1": exp1, "pv": pv,
                      "otT": otT, "onT": onT_, "wo": wo_, "route": route, "ffn": ffn})


_OUTS = [((4, 512, 128), 'float32')]


def kernel(**inputs):
    import numpy as _np
    import concourse.bacc as _bacc
    from concourse import mybir as _mybir
    from concourse.bass_utils import run_bass_kernel_spmd as _run

    a = {k: _np.asarray(t) for k, t in inputs.items()}
    E, F, D = a['L0_ffn_W1'].shape
    w12 = _np.concatenate([a['L0_ffn_W1'], a['L0_ffn_W2']], axis=1).transpose(2, 0, 1)
    w3 = a['L0_ffn_W3'].transpose(2, 0, 1).reshape(F // 128, 128, E, D).transpose(1, 2, 0, 3)
    laid = {
        'x': a['L0_attn_x'], 'w_qkv': a['L0_attn_W_qkv'], 'b_qkv': a['L0_attn_b_qkv'],
        'bqk_t': a['L0_attn_b_qkv'][:2 * D].reshape(2, D).T, 'w_o': a['L0_attn_W_o'],
        'b_o': a['L0_attn_b_o'], 'wg_t': a['L0_ffn_Wg'].T, 'w12_t': w12, 'w3_t': w3,
    }
    nc = _bacc.Bacc("TRN2", target_bir_lowering=False, num_devices=1)
    arrays, args = {}, []
    for name, t in laid.items():
        t = _np.ascontiguousarray(t)
        arrays[f"in_{name}_dram"] = t
        args.append(nc.dram_tensor(f"in_{name}_dram", t.shape, _mybir.dt.from_np(t.dtype), kind="ExternalInput").ap())
    for i, (shape, dtype) in enumerate(_OUTS):
        dt = _mybir.dt.from_np(_np.dtype(dtype))
        args.append(nc.dram_tensor(f"out_{i}_dram", shape, dt, kind="ExternalOutput").ap())
    attention_and_experts(nc, *args)
    r = _run(nc, [arrays], core_ids=[0])
    got = tuple(r.results[0][f"out_{i}_dram"] for i in range(len(_OUTS)))
    return got[0]
```

```python
from contextlib import ExitStack

import concourse.bass as bass
from concourse import mybir

ALU = mybir.AluOpType
ACT = mybir.ActivationFunctionType
AX = mybir.AxisListType
F32 = mybir.dt.float32
BF16 = mybir.dt.bfloat16
I32 = mybir.dt.int32
U32 = mybir.dt.uint32

P = 128
HEADS = 16
DK = 8
QUAD = 4
EXPERTS = 8
TOP = 2
EPS = 1e-5
MASKED = -3.0e38

Q_PART = (0, 0, 0, 1, 1, 2)
K_PART = (0, 1, 2, 0, 1, 0)
TERM_ROWS = len(Q_PART) * DK
SHIFT_ROW = 64
SHIFT_PARTS = 3
VW = 16
ROWS = 96

CHUNKS = (((0, 0, 0),), ((1, 0, 0),), ((0, 1, 0), (0, 3, 384)), ((1, 1, 0), (1, 3, 384)), ((0, 2, 0), (1, 2, 256)))
DIAGONALS = ((0, 5), (1408, 2), (2304, 1))
MAX_GROUPS = tuple((3, c, 1) for c in range(4)) + tuple((2, c, 1) for c in range(4)) + ((1, 0, 2), (1, 2, 2), (0, 0, 4))
NMAX = len(MAX_GROUPS)
NEXP = 2 * len(CHUNKS)


def chunk_of(c, j):
    for n, parts in enumerate(CHUNKS):
        for head, tile, col in parts:
            if (head, tile) == (c % 2, j):
                return 5 * (c // 2) + n, col


LEAD = 22
SHIFT_AT = 3
PV_AT = 6
OT_LAG = 1
SPLIT_AT = (-8, 2, 13)
MAX_FIRST = 2
PLACE_AT = -19
SCATTER_AT = -16
FFN_AT = 40
FFN_STEP = 11
GATHER_LAG = 1
GATHER_STEP = 2
COMBINE_LAG = 8
OT_AT, OT_STEP, WO_AT = 1, 2, 10


def line_of_work(B, TILES, QUADS, UNITS):
    STEPS, NT = B * QUADS, B * TILES
    beside = {}

    def put(at, *work):
        beside.setdefault(at, []).append(work)

    def exp_at(s):
        return NMAX * s - max(0, s + 1 - (STEPS - LEAD // NMAX))

    for s in range(STEPS):
        put(NMAX * (s + 1) - 1 - LEAD + SHIFT_AT, "shift", s)
    for b in range(1, B):
        at = SPLIT_AT[b - 1]
        put(at, "q", b)
        put(at, "k", b)
        put(at + 1, "part", b, 0)
        put(at + 2, "rest", b, 0)
        put(at + 3, "part", b, 1)
        put(at + 4, "rest", b, 1)
        put(at + 4, "bounce", b)
    put(PLACE_AT, "place")
    for n in range(NT * TOP):
        put(SCATTER_AT + n, "scatter", n)
    for s in range(STEPS):
        put(exp_at(s) + NMAX + PV_AT, "pv", s)
        put(exp_at(s) + NMAX + PV_AT + OT_LAG, "ot", s)
    for b in range(B - 1):
        at = NMAX * (QUADS * (b + 1) + 1)
        for i in range(TILES):
            put(at + OT_AT + OT_STEP * i, "otT", b, i)
        put(at + WO_AT - 1, "onT", b)
        put(at + WO_AT, "wo", b)
    for u in range(UNITS):
        put(FFN_AT + FFN_STEP * u // 5, "ffn", u)
    done = FFN_AT + FFN_STEP * UNITS // 5 + GATHER_LAG
    for t in range(NT):
        if t % TILES == 0:
            put(done + GATHER_STEP * t, "gather", t // TILES)
        added = NMAX * (QUADS * (t // TILES + 1) + 1) + WO_AT + 1 if t < NT - TILES else 0
        put(max(done + GATHER_STEP * t + COMBINE_LAG, added), "combine", t)

    order = [("ln", 0), ("xnT", 0), ("q", 0), ("k", 0), ("part", 0, 0), ("ln", 1), ("rest", 0, 0), ("part", 0, 1), ("xnT", 1),
             ("rest", 0, 1), ("bounce", 0), ("v", 0, 0), ("v", 0, 1), ("ln", 2), ("v", 1, 0), ("v", 1, 1), ("xnT", 2),
             ("ln", 3), ("v", 2, 0), ("v", 2, 1), ("xnT", 3), ("v", 3, 0), ("v", 3, 1)]
    order += [("max1", 0, k) for k in range(MAX_FIRST)] + [("gate",)]
    for at in range(MAX_FIRST - LEAD, max(*beside, NMAX * STEPS) + 1):
        s, k = divmod(at + LEAD, NMAX)
        if s < STEPS:
            order.append(("max1", s, k))
        order += [("exp1", s, at - exp_at(s)) for s in range(STEPS) if 0 <= at - exp_at(s) < NEXP]
        order += beside.get(at, [])
    order += [("otT", B - 1, i) for i in range(TILES)] + [("onT", B - 1), ("wo", B - 1)]
    return order


def attention_and_experts(nc, x, w_qk, w_v, b_v, bqk_t, w_o, b_o, wg_t, w12_t, w3_t, out):
    B, T, D = x.shape
    F = w12_t.shape[2] // 2
    TILES = T // P
    NT = B * TILES
    QUADS = HEADS // QUAD
    STEPS = B * QUADS
    FC = F // P
    SLOTS = NT * P * TOP
    NBLK = SLOTS // P + EXPERTS - 1
    SCALE = float(DK) ** -0.5
    assert D == P and T == 512 and HEADS * DK == D and FC == 2

    with ExitStack() as ctx:
        def sb(name, shape, dt=F32):
            return ctx.enter_context(nc.sbuf_tensor(name, shape, dt))

        def bank(name):
            return ctx.enter_context(nc.psum_tensor(name, [P, 512], F32))

        def sem(name):
            return ctx.enter_context(nc.semaphore(name))

        CLEAR = 6
        SPARE = 3
        OTS = QUADS + 1
        NXS = 8
        qk_dram = nc.dram_tensor("qk_parts_dram", [B, 2, len(Q_PART), P, T], BF16).ap()
        xs_dram = nc.dram_tensor("sorted_x_dram", [NBLK * P, D + 1], F32).ap()
        ys_dram = nc.dram_tensor("pair_y_dram", [SPARE + SLOTS, D], F32).ap()

        wqk = sb("wqk", [P, 2 * D])
        wvg = sb("wvg", [P, D + EXPERTS])
        wo = sb("wo", [P, D])
        w12 = sb("w12", [P, EXPERTS, 2 * F])
        w3 = sb("w3", [P, EXPERTS, FC, D])
        bq = sb("bq", [P, 2])
        bv_row = sb("bv_row", [P, D])
        bo_row = sb("bo_row", [P, D])
        ident = sb("ident", [P, P])
        ident_bf = sb("ident_bf", [P, P], BF16)
        ones_bf = sb("ones_bf", [P, P], BF16)
        before = sb("before", [P, P], BF16)
        future = sb("future", [P, P], BF16)
        iota_e = sb("iota_e", [P, EXPERTS])
        iota_me = sb("iota_me", [P, EXPERTS])
        iota_128 = sb("iota_128", [P, NT])
        iota_blk = sb("iota_blk", [P, NBLK])
        tri_e = sb("tri_e", [P, EXPERTS, EXPERTS])
        zeros = sb("zeros", [P, 512])
        blank = sb("blank", [P, CLEAR, D + 1])
        ones_rows = sb("ones_rows", [SHIFT_PARTS, T], BF16)
        xt = sb("xt", [P, NT, D])
        xn = sb("xn", [P, NT, D + 1])
        xa = sb("xa", [P, NT, D])
        xnT = sb("xnT", [P, B, T])
        stats = sb("stats", [P, NT, 6])
        mv = sb("mv", [P, NT, 2])
        ve = sb("ve", [P, NT])
        sd = sb("sd", [P, NT])
        rstd = sb("rstd", [P, NT])
        early = sb("early", [P, 6 * T])
        qkf = early[:, 0:4 * T].rearrange("p (n w t) -> p n w t", n=2, w=2)
        rest = early[:, 4 * T:6 * T].rearrange("p (w t) -> p w t", w=2)
        parts = sb("parts", [P, 2, 2, 3, T], BF16)
        qkx = sb("qkx", [P, 2, QUADS, QUAD, T], BF16)
        qx, kx = qkx[:, 0], qkx[:, 1]
        v = sb("v", [P, B, TILES, HEADS, VW])
        nmax = sb("nmax", [P, 2, QUAD, TILES])
        nmr_rows = sb("nmr_rows", [TILES * QUAD, 2, P])
        nm_rest = sb("nm_rest", [TILES * QUAD, 2, P])
        nm_parts = sb("nm_parts", [TILES * QUAD, 2, 3, P], BF16)
        probs = sb("probs", [P, 2, NEXP * 512])
        ot = sb("ot", [P, OTS, T])
        rden = sb("rden", [P, TILES, HEADS])
        on = xnT[:, 0, :].rearrange("p (i d) -> p i d", i=TILES)
        onT = xnT[:, 1, :]
        sc = sb("sc", [P, NT, EXPERTS])
        sc2 = sb("sc2", [P, NT, EXPERTS])
        cand = sb("cand", [P, NT, EXPERTS])
        best = sb("best", [P, TOP, NT])
        least = sb("least", [P, TOP, NT])
        onehot = sb("onehot", [P, NT * TOP, EXPERTS], BF16)
        dsc = sb("dsc", [P, NT])
        esc = sb("esc", [P, NT])
        prob = sb("prob", [P, TOP, NT])
        cnt = sb("cnt", [P, EXPERTS], BF16)
        total = sb("total", [P, EXPERTS])
        over = probs[:, 1, 0:EXPERTS * NT].rearrange("p (e t) -> p e t", t=NT)
        rank = probs[:, 1, 512:512 + NT * TOP * EXPERTS].rearrange("p (n e) -> p n e", e=EXPERTS)
        past = probs[:, 1, 1024:1024 + NBLK * EXPERTS].rearrange("p (n e) -> p n e", e=EXPERTS)
        nblk = sb("nblk", [P, EXPERTS])
        first = sb("first", [P, EXPERTS])
        last = sb("last", [P, EXPERTS])
        first128 = sb("first128", [P, EXPERTS])
        tri_t = sb("tri_t", [P, EXPERTS, EXPERTS])
        posf = sb("posf", [P, NT * TOP])
        pos = sb("pos", [P, NT * TOP], U32)
        ebf = sb("ebf", [P, NBLK])
        eb = sb("eb", [P, NBLK], I32)
        xs = sb("xs", [P, NXS, D + 1])
        fx = early[:, 0:3 * 512].rearrange("p (n f) -> p n f", n=3)
        th = sb("th", [P, F])
        hid = sb("hid", [P, 3, F])
        yg = w12[:, :, :].rearrange("p e (n d) -> p (e n) d", d=D)
        acc = early[:, 5 * 512:6 * 512].rearrange("p (n d) -> p n d", n=4)

        SM = [bank(f"SM{i}") for i in range(2)]
        ST = [bank(f"ST{i}") for i in range(2)]
        PO = bank("PO")
        M = bank("M")
        FH = bank("FH")
        FM = bank("FM")

        s_x = [sem(f"x_in{b}") for b in range(B)]
        s_w = sem("wqk_in")
        s_wv = sem("wv_wg_in")
        s_bv = sem("bv_in")
        s_wo = sem("wo_bo_in")
        s_wf = sem("ffn_w_in")
        s_const = sem("const_done")
        s_zero = sem("zeros_done")
        s_blank = sem("spare_rows_written")
        s_fill = sem("qkx_filled")
        s_pc = sem("pool_chain")
        s_dc = sem("dve_chain")
        s_ve = sem("var_done")
        s_sd = sem("sd_done")
        s_xn = sem("xn_done")
        s_xa = sem("x_plus_bo_done")
        s_part = sem("parts_done")
        s_rest = sem("rest_done")
        s_bounce = [sem(f"parts_in_dram{b}") for b in range(B)]
        s_slot = [sem(f"qkx_in{g}") for g in range(QUADS)]
        s_v0 = sem("v_without_bias_done")
        s_v = sem("v_done")
        s_v1 = sem("v_ones_done")
        s_sm = sem("scores_written")
        s_max = sem("max_done")
        s_nm = sem("negmax_parts")
        s_shift = [sem(f"shift_in{g}") for g in range(QUADS)]
        s_st = sem("scoresT_written")
        s_exp = sem("exp_done")
        s_sel = sem("causal_done")
        s_poz = sem("pv_cleared")
        s_po = sem("pv_written")
        s_ot = sem("pv_read")
        s_oh = sem("onehot_done")
        s_ds = sem("score_gap_done")
        s_es = sem("score_gap_exp")
        s_rank = sem("rank_written")
        s_pos = sem("pos_done")
        s_eb = sem("block_expert_done")
        s_xz = sem("sorted_x_cleared")
        s_xs_out = [sem(f"sorted_x_out{i}") for i in range(4)]
        s_xs = [sem(f"block_in{i}") for i in range(NXS)]
        s_f1 = sem("ffn_mid_written")
        s_fx = sem("ffn_mid_read")
        s_fh = sem("h_written")
        s_th = sem("tanh_done")
        s_hid = sem("hidden_done")
        s_ys = [sem(f"y_out{i}") for i in range(3)]
        s_yg = [sem(f"y_in{b}") for b in range(B)]
        s_acc = sem("last_batch_experts_added")
        s_res = sem("result_done")
        s_out = sem("out_written")

        UNITS = NBLK + 4
        order = line_of_work(B, TILES, QUADS, UNITS)
        EARLY_KINDS = ("xnT", "q", "k", "v")
        SPREAD = (M, PO, FM, FH)
        AT_END = (M, *SM, *ST, FM)

        def last_batch(w):
            return w[0] in ("otT", "onT", "wo") and w[1] == B - 1

        bank_of, turn, uses = {}, {}, {}
        misc = [w for w in order if w[0] in (*EARLY_KINDS, "shift", "otT", "onT", "wo")]
        for n, w in enumerate(misc):
            if w[0] in ("q", "k") and w[1] > 0:
                home = FM if w[0] == "q" else M
            elif w[0] in EARLY_KINDS:
                home = SPREAD[n % len(SPREAD)]
            else:
                home = AT_END[n % len(AT_END)] if last_batch(w) else M
            bank_of[w] = home
            turn[w] = uses.get(home.name, 0)
            uses[home.name] = turn[w] + 1
        early_uses = {b.name: sum(1 for w in misc if w[0] in EARLY_KINDS and bank_of[w] is b) for b in SPREAD}
        s_m = {b.name: sem(f"written_{b.name}") for b in (*SPREAD, *SM, *ST)}
        s_mf = {b.name: sem(f"read_{b.name}") for b in (*SPREAD, *SM, *ST)}

        def written(*w):
            return s_m[bank_of[w].name], turn[w] + 1

        def read(*w):
            return s_mf[bank_of[w].name], turn[w] + 1

        def in_order(table):
            for w in order:
                if w[0] in table:
                    table[w[0]](*w[1:])

        x_v = x.rearrange("b (t p) d -> p b t d", p=P)
        out_v = out.rearrange("b (t p) d -> p (b t) d", p=P)
        block = ctx.enter_context(nc.Block())

        @block.sync
        def _(sp):
            def x_in(b):
                sp.dma_start(xt[:, TILES * b:TILES * (b + 1), :], x_v[:, b]).then_inc(s_x[b], 16)

            x_in(0)
            sp.dma_start(wvg[:, 0:D], w_v).then_inc(s_wv, 16)
            sp.dma_start(wvg[:, D:D + EXPERTS], wg_t).then_inc(s_wv, 16)
            x_in(1)
            sp.dma_start(bv_row[:, :], b_v.rearrange("(a d) -> a d", a=1).to_broadcast([P, D])).then_inc(s_bv, 16)
            x_in(2)
            x_in(3)
            sp.dma_start(bo_row[:, :], b_o.rearrange("(a d) -> a d", a=1).to_broadcast([P, D])).then_inc(s_wo, 16)
            sp.dma_start(wo[:, :], w_o).then_inc(s_wo, 16)
            sp.wait_ge(s_zero, 2)
            zero_bf = zeros[:, None, :].bitcast(BF16)
            for rows, dst, src in ((slice(TERM_ROWS, ROWS), qx, zero_bf), (slice(TERM_ROWS, SHIFT_ROW), kx, zero_bf),
                                   (slice(SHIFT_ROW + SHIFT_PARTS, ROWS), kx, zero_bf)):
                n = rows.stop - rows.start
                sp.dma_start(dst[rows].rearrange("p g (a c) t -> p (g a) (c t)", c=2),
                             src[rows].to_broadcast([n, QUADS * QUAD // 2, 2 * T])).then_inc(s_fill, 16)
            sp.dma_start(kx[SHIFT_ROW:SHIFT_ROW + SHIFT_PARTS].rearrange("p g c t -> p (g c) t"),
                         ones_rows[:, None, :].to_broadcast([SHIFT_PARTS, QUADS * QUAD, T])).then_inc(s_fill, 16)

            def to_dram(b, w, part, first, n):
                src = parts[:, b % 2, w, part:part + n, :] if part != part_of(w, first + n - 1) else (
                    parts[:, b % 2, w, part:part + 1, :].to_broadcast([P, n, T]))
                sp.dma_start(qk_dram[b, w, first:first + n].rearrange("n p t -> p n t"), src).then_inc(s_bounce[b], 16)

            def part_of(w, term):
                return (Q_PART, K_PART)[w][term]

            def part(b, n):
                sp.wait_ge(s_part, 4 * b + 2 * n + 2)
                if n == 0:
                    to_dram(b, 0, 0, 0, 3)
                    to_dram(b, 1, 0, 5, 1)
                else:
                    to_dram(b, 0, 1, 3, 2)
                    to_dram(b, 1, 0, 3, 2)

            def quad_in(s):
                b, g = s // QUADS, s % QUADS
                if s >= QUADS:
                    sp.wait_ge(s_st, NEXP * (s - QUADS + 1))
                if g == 0:
                    sp.wait_ge(s_bounce[b], 16 * 6)
                if s >= QUADS:
                    sp.dma_start(qx[SHIFT_ROW:SHIFT_ROW + SHIFT_PARTS, g].rearrange("p (a c) t -> p a (c t)", c=2),
                                 zeros[0:SHIFT_PARTS, None, :].bitcast(BF16).to_broadcast([SHIFT_PARTS, QUAD // 2, 2 * T])
                                 ).then_inc(s_slot[g], 16)
                src = qk_dram[b].rearrange("w n (d h) t -> (n d) w h t", h=HEADS)
                sp.dma_start(qkx[0:TERM_ROWS, :, g], src[:, :, QUAD * g:QUAD * (g + 1)]).then_inc(s_slot[g], 16)

            def shift(s):
                g = s % QUADS
                sp.wait_ge(s_nm, s + 1)
                for a in range(SHIFT_PARTS):
                    sp.dma_start(qx[SHIFT_ROW + a:SHIFT_ROW + a + 1, g].rearrange("p c (i j) -> p (c i) j", j=P),
                                 nm_parts[:, s % 2, a, :]).then_inc(s_shift[g], 16)

            def block_in(n):
                if n == 0:
                    for done in s_xs_out:
                        sp.wait_ge(done, 16 * NT * TOP // 4)
                if n >= NXS:
                    u = n - NXS + 4
                    sp.wait_ge(s_ys[u % 3], 16 * len(range(4 + (u - 4) % 3, u + 1, 3)))
                sp.dma_start(xs[:, n % NXS, :], xs_dram[n * P:(n + 1) * P, :]).then_inc(s_xs[n % NXS], 16)

            def ffn(u):
                if u == 0:
                    for n in range(3):
                        block_in(n)
                if u + 3 < NBLK:
                    block_in(u + 3)

            def parts_out(b):
                sp.wait_ge(s_rest, 4 * b + 4)
                to_dram(b, 0, 2, 5, 1)
                to_dram(b, 1, 0, 0, 3)
                if b == 0:
                    for s in range(QUADS):
                        quad_in(s)
                    sp.wait_ge(s_blank, 1)
                    for n in range(0, NBLK, CLEAR):
                        m = min(CLEAR, NBLK - n)
                        sp.dma_start(xs_dram[n * P:(n + m) * P, :].rearrange("(r p) d -> p r d", p=P),
                                     blank[:, 0:m, :]).then_inc(s_xz, 16)
                    sp.dma_start(w12[:, :, :], w12_t).then_inc(s_wf, 16)
                    sp.dma_start(w3[:, :, :, :], w3_t).then_inc(s_wf, 16)

            def exp1(s, k):
                if k == 2 and s >= 1 and s + QUADS - 1 < STEPS:
                    quad_in(s + QUADS - 1)

            def gather(b):
                if b == 0:
                    for i in range(3):
                        sp.wait_ge(s_ys[i], 16 * len([u for u in range(4, UNITS) if u % 3 == i]))
                pairs = ys_dram[SPARE:SPARE + SLOTS].rearrange("(t p c) d -> p t (c d)", p=P, c=TOP)
                ts = slice(TILES * b, TILES * (b + 1))
                sp.dma_start(yg[:, TOP * TILES * b:TOP * TILES * (b + 1), :].rearrange("p (t c) d -> p t (c d)", c=TOP),
                             pairs[:, ts]).then_inc(s_yg[b], 16)

            def rows_out(b):
                sp.wait_ge(s_res, TILES * (b + 1) if b < B - 1 else TILES * (B - 1) + 1)
                ts = slice(TILES * b, TILES * (b + 1))
                sp.dma_start(out_v[:, ts, :], xt[:, ts, :]).then_inc(s_out, 16)

            def combine(t):
                if t % TILES == TILES - 1 and t < NT - TILES:
                    rows_out(t // TILES)

            in_order({"part": part, "bounce": parts_out, "shift": shift, "exp1": exp1, "ffn": ffn, "gather": gather,
                      "combine": combine})
            rows_out(B - 1)
            sp.wait_ge(s_out, 16 * B)

        @block.gpsimd
        def _(pool):
            n_chain = [0]

            def link(ins):
                n_chain[0] += 1
                ins.then_inc(s_pc, 1)
                pool.wait_ge(s_pc, n_chain[0])

            g = nc.gpsimd
            link(g.memset(ident[:], 0.0))
            g.affine_select(out=ident[:], in_=ident[:], compare_op=ALU.not_equal, fill=1.0, base=0,
                            pattern=[[-1, P]], channel_multiplier=1).then_inc(s_const, 1)

            pool.wait_ge(s_const, 1)
            g.tensor_copy(ident_bf[:], ident[:]).then_inc(s_const, 1)
            link(g.memset(future[:], 0.0))
            g.affine_select(out=future[:], in_=future[:], compare_op=ALU.is_ge, fill=MASKED, base=0,
                            pattern=[[-1, P]], channel_multiplier=1).then_inc(s_const, 1)

            g.memset(v[:].rearrange("p a b c d -> p (a b c) d")[:, :, DK + 1:VW], 0.0)
            g.memset(v[:].rearrange("p a b c d -> p (a b c) d")[:, :, DK:DK + 1], 1.0).then_inc(s_v1, 1)
            link(g.memset(before[:], 1.0))
            g.affine_select(out=before[:], in_=before[:], compare_op=ALU.is_gt, fill=0.0, base=0,
                            pattern=[[1, P]], channel_multiplier=-1).then_inc(s_const, 1)
            g.iota(iota_e[:], [[1, EXPERTS]], base=0, channel_multiplier=0, allow_small_or_imprecise_dtypes=True)
            g.iota(iota_me[:], [[1, EXPERTS]], base=-EXPERTS, channel_multiplier=0, allow_small_or_imprecise_dtypes=True)
            g.iota(iota_128[:], [[P, NT]], base=0, channel_multiplier=0, allow_small_or_imprecise_dtypes=True)
            g.iota(iota_blk[:], [[1, NBLK]], base=0, channel_multiplier=0, allow_small_or_imprecise_dtypes=True)
            link(g.memset(tri_e[:], 1.0))
            g.affine_select(out=tri_e[:], in_=tri_e[:], compare_op=ALU.is_gt, fill=0.0, base=0,
                            pattern=[[1, EXPERTS], [-1, EXPERTS]], channel_multiplier=0).then_inc(s_const, 1)

            def result_rows(c, half):
                ts = slice(NT // 2 * half, NT // 2 * (half + 1))
                link(g.iota(xn[:, ts, D:D + 1].rearrange("p t a -> p (t a)").bitcast(I32), [[TOP * P, NT // 2]],
                            base=SPARE + c + TOP * P * ts.start, channel_multiplier=TOP))

            for half in range(2):
                result_rows(0, half)
            pool.wait_ge(s_zero, 3)
            g.iota(blank[:, :, D:D + 1].rearrange("p r a -> p (r a)").bitcast(I32), [[0, CLEAR // SPARE], [1, SPARE]], base=0,
                   channel_multiplier=0).then_inc(s_blank, 1)

            def causal(s, pair):
                pool.wait_ge(s_exp, NEXP * s + 5 * (pair + 1))
                for at, n in DIAGONALS:
                    base = 2560 * pair + at - at % 512
                    banks = probs[:, s % 2, base:base + 512 * n].rearrange("p (a b) -> p a b", b=512)
                    view = banks[:, :, at % 512:at % 512 + P]
                    ins = g.affine_select(out=view, in_=view, compare_op=ALU.is_ge, fill=0.0, base=0,
                                          pattern=[[0, n], [1, P]], channel_multiplier=-1)
                ins.then_inc(s_sel, 1)

            def shift(s):
                r, q = nmr_rows[:, s % 2, :], nm_parts[:, s % 2]
                e = nm_rest[:, s % 2, :]
                pool.wait_ge(*read("shift", s))
                if s >= 2:
                    pool.wait_ge(s_shift[(s - 2) % QUADS], 16 * SHIFT_PARTS * ((s - 2) // QUADS + 1))
                link(g.tensor_scalar(q[:, 0, :], r, 1.0, 0.0, ALU.mult, ALU.add))
                link(g.tensor_tensor(e, r, q[:, 0, :], ALU.subtract))
                link(g.tensor_scalar(q[:, 1, :], e, 1.0, 0.0, ALU.mult, ALU.add))
                g.tensor_tensor(q[:, 2, :], e, q[:, 1, :], ALU.subtract).then_inc(s_nm, 1)

            def scatter(n):
                c, t = n // NT, n % NT
                half = t // (NT // 2)
                if c == 1 and t % (NT // 2) == 0:
                    pool.wait_ge(s_xs_out[half], 16 * NT // 2)
                    result_rows(1, half)
                if n == 0:
                    pool.wait_ge(s_pos, 1)
                    pool.wait_ge(s_xz, 16 * ((NBLK + CLEAR - 1) // CLEAR))
                    pool.wait_ge(s_xn, B)
                place = pos[:, TOP * t + c:TOP * t + c + 1]
                g.indirect_dma_start(out=xs_dram[:, :], out_offset=bass.IndirectOffsetOnAxis(ap=place, axis=0),
                                     in_=xn[:, t, :], in_offset=None).then_inc(s_xs_out[2 * c + half], 16)

            def exp1(s, k):
                if k % 5 == 4:
                    causal(s, k // 5)

            def ffn(u):
                if u >= 4:
                    pool.wait_ge(s_fx, u + 1)
                    rows = xs[:, (u - 4) % NXS, D:D + 1].bitcast(U32)
                    g.indirect_dma_start(out=ys_dram[:, :], out_offset=bass.IndirectOffsetOnAxis(ap=rows, axis=0),
                                         in_=fx[:, u % 3, 384:512], in_offset=None).then_inc(s_ys[u % 3], 16)

            def value_bias(b, half):
                if b == 0 and half == 0:
                    pool.wait_ge(s_bv, 16)
                pool.wait_ge(s_v0, 2 * b + half + 1)
                here = v[:, b, 2 * half:2 * half + 2, :, 0:DK]
                bias = bv_row[:, None, :].rearrange("p a (h d) -> p a h d", d=DK).to_broadcast([P, 2, HEADS, DK])
                g.tensor_tensor(here, here, bias, ALU.add).then_inc(s_v, 1)

            def residual():
                for b in range(B):
                    pool.wait_ge(s_x[b], 16)
                pool.wait_ge(s_wo, 16 * 2)
                g.tensor_tensor(xa[:, :, :], xt[:, :, :], bo_row[:, None, :].to_broadcast([P, NT, D]),
                                ALU.add).then_inc(s_xa, 1)

            in_order({"exp1": exp1, "shift": shift, "scatter": scatter, "v": value_bias, "gate": residual,
                      "ffn": ffn})

        @block.scalar
        def _(act):
            a = nc.scalar
            act.dma_start(wqk[:, :], w_qk).then_inc(s_w, 16)
            act.dma_start(bq[:, :], bqk_t).then_inc(s_w, 16)

            def root(b):
                act.wait_ge(s_ve, b + 1)
                a.activation(sd[:, TILES * b:TILES * (b + 1)], ve[:, TILES * b:TILES * (b + 1)], ACT.Sqrt).then_inc(s_sd, 1)

            def xnT_read(b):
                act.wait_ge(*written("xnT", b))
                home = bank_of["xnT", b]
                a.copy(xnT[:, b, :], home[:, :]).then_inc(s_mf[home.name], 1)

            def v_read(b, half):
                act.wait_ge(*written("v", b, half))
                home = bank_of["v", b, half]
                m = home[:, :].rearrange("p (t c) -> p t c", t=2)
                a.copy(v[:, b, 2 * half:2 * half + 2, :, 0:DK],
                       m[:, :, 0:D].rearrange("p t (h d) -> p t h d", d=DK)).then_inc(s_v0, 1)
                t = TILES * b + 2 * half
                a.copy(sc[:, t:t + 2, :], m[:, :, D:D + EXPERTS]).then_inc(s_mf[home.name], 1)

            def part(b, n):
                for w in range(2):
                    if n == 0:
                        act.wait_ge(*read(("q", "k")[w], b))
                        if b >= 2:
                            act.wait_ge(s_bounce[b - 2], 16 * 6)
                        a.copy(parts[:, b % 2, w, 0, :], qkf[:, b % 2, w]).then_inc(s_part, 1)
                    else:
                        act.wait_ge(s_rest, 4 * b + w + 1)
                        a.copy(parts[:, b % 2, w, 1, :], rest[:, w, :]).then_inc(s_part, 1)

            def exp1(s, k):
                n = NEXP * s + k
                act.wait_ge(s_st, n + 1)
                if s >= 2 and k == 0:
                    act.wait_ge(s_po, s - 1)
                a.activation(probs[:, s % 2, 512 * k:512 * (k + 1)], ST[n % 2][:, :], ACT.Exp).then_inc(s_exp, 1)

            def ot_read(s):
                act.wait_ge(s_po, s + 1)
                if s >= OTS:
                    act.wait_ge(*written("otT", (s - OTS) // QUADS, TILES - 1))
                a.copy(ot[:, s % OTS, :], PO[:, :]).then_inc(s_ot, 1)

            def ffn(u):
                if u == 0:
                    act.wait_ge(s_rest, 4 * B)
                act.wait_ge(s_f1, u + 1)
                if u >= 7:
                    act.wait_ge(s_ys[u % 3], 16 * len(range(4 + (u - 4) % 3, u, 3)))
                a.copy(fx[:, u % 3, :], FM[:, :]).then_inc(s_fx, 1)

                if 1 <= u <= NBLK:
                    act.wait_ge(s_fh, u)
                    if u >= 2:
                        act.wait_ge(s_hid, u - 1)
                    a.activation(th[:, :], FH[:, 0:F], ACT.Tanh, scale=0.5).then_inc(s_th, 1)

            def gap_exp():
                act.wait_ge(s_ds, 1)
                a.activation(esc[:, :], dsc[:, :], ACT.Exp).then_inc(s_es, 1)

            def onT_read(b):
                act.wait_ge(*written("onT", b))
                home = bank_of["onT", b]
                a.copy(onT[:, :], home[:, :]).then_inc(s_mf[home.name], 1)

            in_order({"ln": root, "xnT": xnT_read, "v": v_read, "part": part, "exp1": exp1, "ot": ot_read, "ffn": ffn,
                      "gate": gap_exp, "onT": onT_read})

        @block.vector
        def _(dve):
            e = nc.vector
            n_chain = [0]

            def link(ins):
                n_chain[0] += 1
                ins.then_inc(s_dc, 1)
                dve.wait_ge(s_dc, n_chain[0])

            e.memset(zeros[:], 0.0).then_inc(s_zero, 1)
            e.memset(ones_rows[:], 1.0).then_inc(s_zero, 1)
            e.memset(blank[:], 0.0).then_inc(s_zero, 1)

            def layer_norm(b):
                ts = slice(TILES * b, TILES * (b + 1))
                dve.wait_ge(s_x[b], 16)
                for t in range(TILES * b, TILES * (b + 1)):
                    ins = e.bn_stats(stats[:, t, :], xt[:, t, :])
                link(ins)
                for t in range(TILES * b, TILES * (b + 1)):
                    ins = e.bn_aggr(mv[:, t, :], stats[:, t, :])
                link(ins)
                e.tensor_scalar(ve[:, ts], mv[:, ts, 1], EPS, None, ALU.add).then_inc(s_ve, 1)
                dve.wait_ge(s_sd, b + 1)
                link(e.reciprocal(rstd[:, ts], sd[:, ts]))
                for t in range(TILES * b, TILES * (b + 1)):
                    ins = e.tensor_scalar(xn[:, t, 0:D], xt[:, t, :], mv[:, t, 0:1], rstd[:, t:t + 1], ALU.subtract, ALU.mult)
                ins.then_inc(s_xn, 1)
                if b == 0:
                    e.memset(ones_bf[:], 1.0)
                    e.memset(PO[:, :], 0.0).then_inc(s_poz, 1)

            def q_read(b):
                dve.wait_ge(*written("q", b))
                if b == 0:
                    dve.wait_ge(s_w, 16 * 2)
                if b >= 2:
                    dve.wait_ge(s_rest, 4 * (b - 2) + 2)
                home = bank_of["q", b]
                e.tensor_scalar(qkf[:, b % 2, 0, :], home[:, :], bq[:, 0:1], SCALE, ALU.add,
                                ALU.mult).then_inc(s_mf[home.name], 1)

            def k_read(b):
                dve.wait_ge(*written("k", b))
                home = bank_of["k", b]
                e.tensor_scalar(qkf[:, b % 2, 1, :], home[:, :], bq[:, 1:2], None, ALU.add).then_inc(s_mf[home.name], 1)

            def max1(s, k):
                n = NMAX * s + k
                i, c, heads = MAX_GROUPS[k]
                dve.wait_ge(s_sm, n + 1)
                if k == 0 and s >= 2:
                    dve.wait_ge(*written("shift", s - 2))
                w = P * (i + 1)
                e.tensor_reduce(nmax[:, s % 2, c:c + heads, i], SM[n % 2][:, 0:heads * w].rearrange("p (c w) -> p c w", w=w),
                                AX.X, ALU.max, negate=True).then_inc(s_max, 1)

            def shift(s):
                dve.wait_ge(*written("shift", s))
                if s >= 2:
                    dve.wait_ge(s_nm, s - 1)
                home = bank_of["shift", s]
                e.tensor_copy(nmr_rows[:, s % 2, :], home[0:TILES * QUAD, 0:P]).then_inc(s_mf[home.name], 1)

            def otT(b, i):
                dve.wait_ge(*written("otT", b, i))
                home = bank_of["otT", b, i]
                m = home[:, :].rearrange("p (h r) -> p h r", r=32)
                link(e.reciprocal(rden[:, i, :], m[:, :, DK]))
                if b:
                    dve.wait_ge(*written("onT", b - 1))
                e.tensor_tensor(on[:, i, :].rearrange("p (h d) -> p h d", d=DK), m[:, :, 0:DK],
                                rden[:, i, :, None].to_broadcast([P, HEADS, DK]), ALU.mult).then_inc(s_mf[home.name], 1)

            def wo_read(b):
                dve.wait_ge(*written("wo", b))
                dve.wait_ge(s_xa, 1)
                ts = slice(TILES * b, TILES * (b + 1))
                home = bank_of["wo", b]
                m = home[:, :].rearrange("p (t d) -> p t d", d=D)
                if b == B - 1:
                    dve.wait_ge(s_res, NT - TILES)
                    dve.wait_ge(s_acc, TILES)
                    e.tensor_tensor(xt[:, ts, :], m, xa[:, ts, :], ALU.add).then_inc(s_res, 1)
                else:
                    e.tensor_tensor(xa[:, ts, :], m, xa[:, ts, :], ALU.add).then_inc(s_mf[home.name], 1)

            def combine(t):
                dve.wait_ge(s_yg[t // TILES], 16)
                dve.wait_ge(s_xa, 1)
                if t < NT - TILES:
                    dve.wait_ge(*read("wo", t // TILES))
                link(e.scalar_tensor_tensor(out=acc[:, t % 4, :], in0=yg[:, TOP * t, :], scalar=prob[:, 0, t:t + 1],
                                            in1=xa[:, t, :], op0=ALU.mult, op1=ALU.add))
                last_batch = t >= NT - TILES
                e.scalar_tensor_tensor(out=(xa if last_batch else xt)[:, t, :], in0=yg[:, TOP * t + 1, :],
                                       scalar=prob[:, 1, t:t + 1], in1=acc[:, t % 4, :], op0=ALU.mult,
                                       op1=ALU.add).then_inc(s_acc if last_batch else s_res, 1)

            def ffn(u):
                if 1 <= u <= NBLK:
                    n = u - 1
                    dve.wait_ge(s_th, u)
                    link(e.scalar_tensor_tensor(out=th[:, :], in0=th[:, :], scalar=1.0, in1=FH[:, 0:F],
                                                op0=ALU.add, op1=ALU.mult))
                    if n >= 3:
                        dve.wait_ge(s_f1, n + 1)
                    e.scalar_tensor_tensor(out=hid[:, n % 3, :], in0=th[:, :], scalar=0.5, in1=FH[:, F:2 * F],
                                           op0=ALU.mult, op1=ALU.mult).then_inc(s_hid, 1)

            def gate():
                dve.wait_ge(s_const, 5)
                for half in range(2):
                    dve.wait_ge(*read("v", B - 1, half))
                oh = onehot[:, :, :]
                here = sc[:, :, :]
                for c in range(TOP):
                    chosen = oh.rearrange("p (t c) e -> p t c e", c=TOP)[:, :, c, :]
                    link(e.tensor_reduce(best[:, c, :], here, AX.X, ALU.max))
                    if c == 1:
                        e.tensor_tensor(dsc[:, :], best[:, 1, :], best[:, 0, :], ALU.subtract).then_inc(s_ds, 1)
                    link(e.tensor_tensor(cand[:, :, :], here, best[:, c, :, None].to_broadcast([P, NT, EXPERTS]), ALU.is_equal))
                    link(e.scalar_tensor_tensor(out=cand[:, :, :], in0=cand[:, :, :], scalar=-float(EXPERTS),
                                                in1=iota_e[:, None, :].to_broadcast([P, NT, EXPERTS]), op0=ALU.mult,
                                                op1=ALU.add))
                    link(e.tensor_reduce(least[:, c, :], cand[:, :, :], AX.X, ALU.min))
                    ins = e.tensor_tensor(chosen, least[:, c, :, None].to_broadcast([P, NT, EXPERTS]),
                                          iota_me[:, None, :].to_broadcast([P, NT, EXPERTS]), ALU.is_equal)
                    if c == 0:
                        link(ins)
                        link(e.scalar_tensor_tensor(out=sc2[:, :, :], in0=chosen, scalar=MASKED, in1=here, op0=ALU.mult,
                                                    op1=ALU.add))
                        here = sc2[:, :, :]
                ins.then_inc(s_oh, 1)
                dve.wait_ge(s_oh, 1)
                with nc.allow_low_precision(reason="counts up to 32 are exact"):
                    e.tensor_reduce(cnt[:, :], oh.rearrange("p n e -> p e n"), AX.X, ALU.add).then_inc(s_oh, 1)

            def place():
                dve.wait_ge(s_es, 1)
                link(e.tensor_scalar(dsc[:, :], esc[:, :], 1.0, None, ALU.add))
                link(e.reciprocal(prob[:, 0, :], dsc[:, :]))
                e.tensor_tensor(prob[:, 1, :], prob[:, 0, :], esc[:, :], ALU.mult)
                oh = onehot[:, :, :]
                dve.wait_ge(s_rank, 1)
                link(e.tensor_copy(total[:, :], FH[:, NT * TOP * EXPERTS:NT * TOP * EXPERTS + EXPERTS]))
                link(e.tensor_tensor(over[:, :, :], total[:, :, None].to_broadcast([P, EXPERTS, NT]),
                                     iota_128[:, None, :].to_broadcast([P, EXPERTS, NT]), ALU.is_gt))
                link(e.tensor_reduce(nblk[:, :], over[:, :, :], AX.X, ALU.add))
                link(e.tensor_tensor(tri_t[:, :, :], tri_e[:, :, :], nblk[:, None, :].to_broadcast([P, EXPERTS, EXPERTS]),
                                     ALU.mult))
                link(e.tensor_reduce(first[:, :], tri_t[:, :, :], AX.X, ALU.add))
                e.tensor_tensor(last[:, :], first[:, :], nblk[:, :], ALU.add)
                link(e.tensor_scalar(first128[:, :], first[:, :], float(P), None, ALU.mult))
                link(e.tensor_tensor(rank[:, :, :], FH[:, 0:NT * TOP * EXPERTS].rearrange("p (n e) -> p n e", e=EXPERTS),
                                     first128[:, None, :].to_broadcast([P, NT * TOP, EXPERTS]), ALU.add))
                link(e.tensor_tensor(rank[:, :, :], rank[:, :, :], oh, ALU.mult))
                link(e.tensor_reduce(posf[:, :], rank[:, :, :], AX.X, ALU.add))
                e.tensor_copy(pos[:, :], posf[:, :]).then_inc(s_pos, 1)
                link(e.tensor_tensor(past[:, :, :], iota_blk[:, :, None].to_broadcast([P, NBLK, EXPERTS]),
                                     last[:, None, :].to_broadcast([P, NBLK, EXPERTS]), ALU.is_ge))
                link(e.tensor_reduce(ebf[:, :], past[:, :, :], AX.X, ALU.add))
                e.tensor_scalar(eb[:, :], ebf[:, :], float(EXPERTS - 1), None, ALU.min).then_inc(s_eb, 1)

            def rest_of(b, n):
                for w in range(2):
                    dve.wait_ge(s_part, 4 * b + 2 * n + w + 1)
                    if n == 0:
                        if b:
                            dve.wait_ge(s_rest, 4 * b - 1 + w)
                        e.tensor_tensor(rest[:, w, :], qkf[:, b % 2, w], parts[:, b % 2, w, 0, :],
                                        ALU.subtract).then_inc(s_rest, 1)
                    else:
                        e.tensor_tensor(parts[:, b % 2, w, 2, :], rest[:, w, :], parts[:, b % 2, w, 1, :],
                                        ALU.subtract).then_inc(s_rest, 1)

            in_order({"ln": layer_norm, "q": q_read, "k": k_read, "rest": rest_of, "max1": max1, "shift": shift,
                      "otT": otT, "wo": wo_read, "combine": combine, "ffn": ffn, "gate": gate, "place": place})

        @block.tensor
        def _(pe):
            t_ = nc.tensor

            def my_turn(*w):
                home = bank_of[w]
                if turn[w] > 0:
                    pe.wait_ge(s_mf[home.name], turn[w])
                if last_batch(w):
                    pe.wait_ge(s_max, NMAX * STEPS)
                    pe.wait_ge(s_exp, NEXP * STEPS)
                    pe.wait_ge(s_fx, UNITS)
                return home

            def free_of_early_work(home):
                pe.wait_ge(s_mf[home.name], early_uses[home.name])

            def xnT_(b):
                home = my_turn("xnT", b)
                if b == 0:
                    pe.wait_ge(s_const, 1)
                pe.wait_ge(s_xn, b + 1)
                for i in range(TILES):
                    ins = t_.transpose(home[:, P * i:P * (i + 1)], xn[:, TILES * b + i, 0:D], ident[:, :])
                ins.then_inc(s_m[home.name], 1)

            def q_(b):
                home = my_turn("q", b)
                pe.wait_ge(*read("xnT", b))
                if b == 0:
                    pe.wait_ge(s_w, 16 * 2)
                    pe.wait_ge(s_poz, 1)
                t_.matmul(home[:, :], wqk[:, 0:D], xnT[:, b, :], start=True, stop=True).then_inc(s_m[home.name], 1)

            def k_(b):
                home = my_turn("k", b)
                t_.matmul(home[:, :], wqk[:, D:2 * D], xnT[:, b, :], start=True, stop=True).then_inc(s_m[home.name], 1)

            def v_(b, half):
                home = my_turn("v", b, half)
                pe.wait_ge(*read("xnT", b))
                if b == 0:
                    pe.wait_ge(s_wv, 16 * 2)
                for i in range(2):
                    t = 2 * half + i
                    ins = t_.matmul(home[:, 256 * i:256 * i + D + EXPERTS], xnT[:, b, P * t:P * (t + 1)], wvg[:, :],
                                    start=True, stop=True)
                ins.then_inc(s_m[home.name], 1)

            def max1(s, k):
                n = NMAX * s + k
                g = s % QUADS
                if k == 0:
                    pe.wait_ge(s_slot[g], 16 * (1 + 2 * (s // QUADS)))
                if n == 0:
                    pe.wait_ge(s_fill, 16 * 4)
                    pe.wait_ge(s_const, 3)
                if n >= 2:
                    pe.wait_ge(s_max, n - 1)
                i, c0, heads = MAX_GROUPS[k]
                w = P * (i + 1)
                bank = SM[n % 2]
                for c in range(heads):
                    t_.matmul(bank[:, w * c:w * (c + 1)], qx[0:ROWS, g, c0 + c, P * i:P * (i + 1)],
                              kx[0:ROWS, g, c0 + c, 0:w], start=(c == 0), stop=False, skip_group_check=True)
                for c in range(heads):
                    at = w * c + P * i
                    ins = t_.matmul(bank[:, at:at + P], ident_bf[:, :], future[:, :], start=False, stop=(c == heads - 1),
                                    skip_group_check=True)
                ins.then_inc(s_sm, 1)

            def shift(s):
                home = my_turn("shift", s)
                pe.wait_ge(s_max, NMAX * (s + 1))
                t_.transpose(home[0:TILES * QUAD, 0:P], nmax[:, s % 2, :, :].rearrange("p c i -> p (c i)"),
                             ident[:, :]).then_inc(s_m[home.name], 1)

            def exp1(s, k):
                n = NEXP * s + k
                g = s % QUADS
                if k == 0:
                    pe.wait_ge(s_shift[g], 16 * SHIFT_PARTS * (s // QUADS + 1))
                if n >= 2:
                    pe.wait_ge(s_exp, n - 1)
                for m, (c, j, at) in enumerate(CHUNKS[k % 5]):
                    h = 2 * (k // 5) + c
                    w = T - P * j
                    ins = t_.matmul(ST[n % 2][:, at:at + w], kx[0:ROWS, g, h, P * j:P * (j + 1)],
                                    qx[0:ROWS, g, h, P * j:T], start=(m == 0), stop=True, skip_group_check=True)
                ins.then_inc(s_st, 1)

            def pv(s):
                b, g = s // QUADS, s % QUADS
                pe.wait_ge(s_sel, 2 * (s + 1))
                if s >= 1:
                    pe.wait_ge(s_ot, s)
                if g == 0:
                    pe.wait_ge(s_v, 2 * (b + 1))
                if s == 0:
                    pe.wait_ge(s_v1, 1)
                    free_of_early_work(PO)
                for j in range(TILES):
                    w = T - P * j
                    for c in range(QUAD):
                        n, at = chunk_of(c, j)
                        o = 512 * n + at
                        ins = t_.matmul(PO[32 * c:32 * c + VW, P * j:T], v[:, b, j, QUAD * g + c, :],
                                        probs[:, s % 2, o:o + w], start=(j == 0), stop=(j == TILES - 1))
                ins.then_inc(s_po, 1)

            def otT(b, i):
                home = my_turn("otT", b, i)
                pe.wait_ge(s_ot, QUADS * (b + 1))
                for g in range(QUADS):
                    ins = t_.transpose(home[:, P * g:P * (g + 1)], ot[:, (QUADS * b + g) % OTS, P * i:P * (i + 1)], ident[:, :])
                ins.then_inc(s_m[home.name], 1)

            def onT_(b):
                home = my_turn("onT", b)
                for i in range(TILES):
                    pe.wait_ge(*read("otT", b, i))
                for i in range(TILES):
                    ins = t_.transpose(home[:, P * i:P * (i + 1)], on[:, i, :], ident[:, :])
                ins.then_inc(s_m[home.name], 1)

            def wo_(b):
                home = my_turn("wo", b)
                pe.wait_ge(*read("onT", b))
                if b == 0:
                    pe.wait_ge(s_wo, 16 * 2)
                for i in range(TILES):
                    ins = t_.matmul(home[:, D * i:D * (i + 1)], onT[:, P * i:P * (i + 1)], wo[:, :], start=True, stop=True)
                ins.then_inc(s_m[home.name], 1)

            def route():
                pe.wait_ge(s_oh, 2)
                free_of_early_work(FH)
                N = NT * TOP
                oh = onehot[:, :, :].rearrange("p n e -> p (n e)")
                t_.matmul(FH[:, 0:N * EXPERTS], before[:, :], oh, start=True, stop=False, skip_group_check=True)
                for d in range(1, N):
                    t_.matmul(FH[:, d * EXPERTS:N * EXPERTS], ones_bf[:, :], oh[:, 0:(N - d) * EXPERTS],
                              start=False, stop=(d == N - 1), skip_group_check=True)
                t_.matmul(FH[:, N * EXPERTS:(N + 1) * EXPERTS], ones_bf[:, :], cnt[:, :],
                          start=False, stop=True, skip_group_check=True).then_inc(s_rank, 1)

            expert = {}

            def ffn(u):
                if u == 0:
                    free_of_early_work(FM)
                    pe.wait_ge(s_eb, 1)
                    pe.wait_ge(s_wf, 32)
                if u >= 1:
                    pe.wait_ge(s_fx, u)
                src = xs[:, u % NXS, 0:D]
                if u < NBLK:
                    pe.wait_ge(s_xs[u % NXS], 16 * (u // NXS + 1))
                    ins = t_.transpose(FM[:, 0:P], src, ident[:, :])
                if 3 <= u < NBLK + 3:
                    pe.wait_ge(s_hid, u - 2)
                    h = hid[:, u % 3, :]
                    for c in range(FC):
                        ins = t_.transpose(FM[:, P * (c + 1):P * (c + 2)], h[:, P * c:P * (c + 1)], ident[:, :])
                elif u < 3:
                    for c in range(FC):
                        ins = t_.transpose(FM[:, P * (c + 1):P * (c + 2)], src, ident[:, :])
                if u >= 4:
                    e3 = expert.pop(u - 4)
                    for c in range(FC):
                        ins = t_.matmul(FM[:, 384:512], fx[:, (u - 1) % 3, P * (c + 1):P * (c + 2)],
                                        w3[:, bass.ds(e3, 1), c, :], start=(c == 0), stop=(c == FC - 1), skip_group_check=True)
                else:
                    ins = t_.transpose(FM[:, 384:512], src, ident[:, :])
                ins.then_inc(s_f1, 1)
                if 1 <= u <= NBLK:
                    if u >= 2:
                        pe.wait_ge(s_hid, u - 1)
                    t_.matmul(FH[:, :], fx[:, (u - 1) % 3, 0:P], w12[:, bass.ds(expert[u - 1], 1), :],
                              start=True, stop=True).then_inc(s_fh, 1)
                if u < NBLK:
                    expert[u] = t_.value_load(eb[0:1, u:u + 1], min_val=0, max_val=EXPERTS - 1)

            in_order({"xnT": xnT_, "q": q_, "k": k_, "v": v_, "max1": max1, "shift": shift, "exp1": exp1, "pv": pv,
                      "otT": otT, "onT": onT_, "wo": wo_, "place": route, "ffn": ffn})


_OUTS = [((4, 512, 128), 'float32')]


def kernel(**inputs):
    import numpy as _np
    import concourse.bacc as _bacc
    from concourse import mybir as _mybir
    from concourse.bass_utils import run_bass_kernel_spmd as _run

    a = {k: _np.asarray(t) for k, t in inputs.items()}
    E, F, D = a['L0_ffn_W1'].shape
    w12 = _np.concatenate([a['L0_ffn_W1'], a['L0_ffn_W2']], axis=1).transpose(2, 0, 1)
    w3 = a['L0_ffn_W3'].transpose(2, 0, 1).reshape(F // 128, 128, E, D).transpose(1, 2, 0, 3)
    w_qk = a['L0_attn_W_qkv'][:, :2 * D].reshape(D, 2, HEADS, DK).transpose(0, 1, 3, 2).reshape(D, 2 * D)
    b_qk = a['L0_attn_b_qkv'][:2 * D].reshape(2, HEADS, DK).transpose(2, 1, 0).reshape(D, 2)
    laid = {
        'x': a['L0_attn_x'], 'w_qk': w_qk, 'w_v': a['L0_attn_W_qkv'][:, 2 * D:], 'b_v': a['L0_attn_b_qkv'][2 * D:],
        'bqk_t': b_qk, 'w_o': a['L0_attn_W_o'],
        'b_o': a['L0_attn_b_o'], 'wg_t': a['L0_ffn_Wg'].T, 'w12_t': w12, 'w3_t': w3,
    }
    nc = _bacc.Bacc("TRN2", target_bir_lowering=False, num_devices=1)
    arrays, args = {}, []
    for name, t in laid.items():
        t = _np.ascontiguousarray(t)
        arrays[f"in_{name}_dram"] = t
        args.append(nc.dram_tensor(f"in_{name}_dram", t.shape, _mybir.dt.from_np(t.dtype), kind="ExternalInput").ap())
    for i, (shape, dtype) in enumerate(_OUTS):
        dt = _mybir.dt.from_np(_np.dtype(dtype))
        args.append(nc.dram_tensor(f"out_{i}_dram", shape, dt, kind="ExternalOutput").ap())
    attention_and_experts(nc, *args)
    r = _run(nc, [arrays], core_ids=[0])
    got = tuple(r.results[0][f"out_{i}_dram"] for i in range(len(_OUTS)))
    return got[0]
```
